# Optimizing a Trainium2 kernel written in Bass

```python
import numpy as np
import jax
import jax.numpy as jnp

def _softmax(x, axis=-1):
    return jax.nn.softmax(x, axis=axis)

def _gelu(x):
    return jax.nn.gelu(x, approximate=True)

def _silu(x):
    return jax.nn.silu(x)

def _sigmoid(x):
    return jax.nn.sigmoid(x)

def _layernorm(x, axis=-1, eps=1e-05):
    m = jnp.mean(x, axis=axis, keepdims=True)
    v = jnp.var(x, axis=axis, keepdims=True)
    return (x - m) / jnp.sqrt(v + eps)

def _scatter_add(tgt, idx, src, axis=0):
    return tgt.at[idx].add(src)

def _segment_sum(src, seg, n):
    return jax.ops.segment_sum(src, seg, n)
kernel_name = 'mk_perceiver_d1_seqx_r8_028884'

def setup_inputs(seed: int=0):
    np.random.seed(seed)
    _w = jnp.asarray

    def _rec_inputs():
        import jax
        import jax.numpy as jnp
        _rk = jax.random.key(seed)
        x = -0.0002928 + 1 * jax.random.normal(jax.random.fold_in(_rk, 1), (1, 64, 128), jnp.float32)
        _lenS = 64 - jax.random.randint(jax.random.fold_in(_rk, 7), (1,), 0, max(1, 64 // 4) + 1, jnp.int32)
        _lenS2 = 6272 - jax.random.randint(jax.random.fold_in(_rk, 8), (1,), 0, max(1, 6272 // 4) + 1, jnp.int32)
        _ctx_1024P = jax.random.normal(jax.random.fold_in(_rk, 11), (1, 16, 128), jnp.float32)
        _ctx_1024c = jax.random.dirichlet(jax.random.fold_in(_rk, 511), 0.3 * jnp.ones((16,), jnp.float32), (1, 6272))
        _ctx_1024t = jnp.einsum('bsk,bkd->bsd', _ctx_1024c, _ctx_1024P)
        _ctx_1024t = _ctx_1024t * jax.lax.rsqrt(jnp.mean(jnp.square(_ctx_1024t)) + 1e-12) * 0.953939
        ctx_1024 = -1.39393e-06 + 0.999914 * (_ctx_1024t + 0.3 * jax.random.normal(jax.random.fold_in(_rk, 611), (1, 6272, 128), jnp.float32))
        return (x, ctx_1024)
    x, ctx_1024 = _rec_inputs()

    def _L0_xattn_setup():
        import jax, jax.numpy as jnp
        import numpy as np
        import math
        EMBED_DIM = 128
        NUM_HEADS = 16
        HEAD_DIM = EMBED_DIM // NUM_HEADS
        SUB_HEAD_DIM = HEAD_DIM // 2
        SCALING = 1.0 / math.sqrt(SUB_HEAD_DIM)
        LAMBDA_INIT = 0.8 - 0.6 * math.exp(-0.3 * 0)
        key = jax.random.key(seed)
        ks = jax.random.split(key, 10)
        B, T, D = (2, 256, EMBED_DIM)
        xav = math.sqrt(6.0 / (D + D))
        return {'query': jax.random.normal(ks[0], (B, T, D), jnp.float32), 'key': jax.random.normal(ks[1], (B, T, D), jnp.float32), 'value': jax.random.normal(ks[2], (B, T, D), jnp.float32), 'in_proj_weight': jax.random.uniform(ks[3], (3 * D, D), jnp.float32, -xav, xav), 'in_proj_bias': jnp.zeros((3 * D,), jnp.float32), 'out_proj_weight': jax.random.uniform(ks[4], (D, D), jnp.float32, -xav, xav), 'out_proj_bias': jnp.zeros((D,), jnp.float32), 'lambda_q1': 0.1 * jax.random.normal(ks[5], (SUB_HEAD_DIM,), jnp.float32), 'lambda_k1': 0.1 * jax.random.normal(ks[6], (SUB_HEAD_DIM,), jnp.float32), 'lambda_q2': 0.1 * jax.random.normal(ks[7], (SUB_HEAD_DIM,), jnp.float32), 'lambda_k2': 0.1 * jax.random.normal(ks[8], (SUB_HEAD_DIM,), jnp.float32)}
    _L0_xattn_all = _L0_xattn_setup()
    _L0_xattn_in = {k: v for k, v in _L0_xattn_all.items() if k in ('in_proj_weight', 'in_proj_bias', 'out_proj_weight', 'out_proj_bias', 'lambda_q1', 'lambda_k1', 'lambda_q2', 'lambda_k2')}
    del _L0_xattn_all

    def _L0_attn_setup():
        import jax, jax.numpy as jnp
        import numpy as np
        import math
        D_MODEL = 128
        N_HEADS = 16
        D_K = D_MODEL // N_HEADS
        NUM_BUCKETS = 32
        MAX_DISTANCE = 128
        BIDIRECTIONAL = True

        def _relative_position_bucket(relative_position):
            num_buckets = NUM_BUCKETS
            ret = jnp.zeros_like(relative_position)
            n = -relative_position
            if BIDIRECTIONAL:
                num_buckets //= 2
                ret = ret + (n < 0).astype(jnp.int32) * num_buckets
                n = jnp.abs(n)
            else:
                n = jnp.maximum(n, 0)
            max_exact = num_buckets // 2
            is_small = n < max_exact
            val_if_large = max_exact + (jnp.log(jnp.maximum(n, 1).astype(jnp.float32) / max_exact) / math.log(MAX_DISTANCE / max_exact) * (num_buckets - max_exact)).astype(jnp.int32)
            val_if_large = jnp.minimum(val_if_large, num_buckets - 1)
            return ret + jnp.where(is_small, n, val_if_large)

        def _position_bias(seq_len, rel_bias_table):
            pos = jnp.arange(seq_len, dtype=jnp.int32)
            relative_position = pos[None, :] - pos[:, None]
            buckets = _relative_position_bucket(relative_position)
            values = rel_bias_table[buckets]
            return jnp.transpose(values, (2, 0, 1))
        key = jax.random.key(seed)
        ks = jax.random.split(key, 6)
        scale = 1.0 / math.sqrt(D_MODEL)
        x = jax.random.normal(ks[0], (2, 256, D_MODEL), dtype=jnp.float32)
        w_q = jax.random.normal(ks[1], (D_MODEL, D_MODEL), dtype=jnp.float32) * scale
        w_k = jax.random.normal(ks[2], (D_MODEL, D_MODEL), dtype=jnp.float32) * scale
        w_v = jax.random.normal(ks[3], (D_MODEL, D_MODEL), dtype=jnp.float32) * scale
        w_o = jax.random.normal(ks[4], (D_MODEL, D_MODEL), dtype=jnp.float32) * scale
        rel_bias_table = jax.random.normal(ks[5], (NUM_BUCKETS, N_HEADS), dtype=jnp.float32) * 0.1
        return {'x': x, 'w_q': w_q, 'w_k': w_k, 'w_v': w_v, 'w_o': w_o, 'rel_bias_table': rel_bias_table}
    _L0_attn_all = _L0_attn_setup()
    _L0_attn_in = {k: v for k, v in _L0_attn_all.items() if k in ('w_q', 'w_k', 'w_v', 'w_o', 'rel_bias_table')}
    del _L0_attn_all

    def _L0_ffn_setup():
        import jax, jax.numpy as jnp
        import numpy as np
        B, T, C, E, K, CAP, H = (8, 256, 128, 8, 2, 512, 512)
        key = jax.random.key(seed)
        ks = jax.random.split(key, 6)
        s = 0.02
        return {'x': jax.random.normal(ks[0], (B, T, C), jnp.float32), 'rw1': s * jax.random.normal(ks[1], (C, H), jnp.float32), 'rb1': jnp.zeros((H,), jnp.float32), 'rw2': s * jax.random.normal(ks[2], (H, E), jnp.float32), 'rb2': jnp.zeros((E,), jnp.float32), 'ew1': s * jax.random.normal(ks[3], (E, C, H), jnp.float32), 'eb1': jnp.zeros((E, H), jnp.float32), 'ew2': s * jax.random.normal(ks[4], (E, H, C), jnp.float32), 'eb2': jnp.zeros((E, C), jnp.float32)}
    _L0_ffn_all = _L0_ffn_setup()
    _L0_ffn_in = {k: v for k, v in _L0_ffn_all.items() if k in ('rw1', 'rb1', 'rw2', 'rb2', 'ew1', 'eb1', 'ew2', 'eb2')}
    del _L0_ffn_all
    return {'x': x, 'ctx_1024': ctx_1024, 'L0_xattn_in_proj_weight': _L0_xattn_in['in_proj_weight'], 'L0_xattn_in_proj_bias': _L0_xattn_in['in_proj_bias'], 'L0_xattn_out_proj_weight': _L0_xattn_in['out_proj_weight'], 'L0_xattn_out_proj_bias': _L0_xattn_in['out_proj_bias'], 'L0_xattn_lambda_q1': _L0_xattn_in['lambda_q1'], 'L0_xattn_lambda_k1': _L0_xattn_in['lambda_k1'], 'L0_xattn_lambda_q2': _L0_xattn_in['lambda_q2'], 'L0_xattn_lambda_k2': _L0_xattn_in['lambda_k2'], 'L0_attn_w_q': _L0_attn_in['w_q'], 'L0_attn_w_k': _L0_attn_in['w_k'], 'L0_attn_w_v': _L0_attn_in['w_v'], 'L0_attn_w_o': _L0_attn_in['w_o'], 'L0_attn_rel_bias_table': _L0_attn_in['rel_bias_table'], 'L0_ffn_rw1': _L0_ffn_in['rw1'], 'L0_ffn_rb1': _L0_ffn_in['rb1'], 'L0_ffn_rw2': _L0_ffn_in['rw2'], 'L0_ffn_rb2': _L0_ffn_in['rb2'], 'L0_ffn_ew1': _L0_ffn_in['ew1'], 'L0_ffn_eb1': _L0_ffn_in['eb1'], 'L0_ffn_ew2': _L0_ffn_in['ew2'], 'L0_ffn_eb2': _L0_ffn_in['eb2']}

def reference(x, ctx_1024, L0_xattn_in_proj_weight, L0_xattn_in_proj_bias, L0_xattn_out_proj_weight, L0_xattn_out_proj_bias, L0_xattn_lambda_q1, L0_xattn_lambda_k1, L0_xattn_lambda_q2, L0_xattn_lambda_k2, L0_attn_w_q, L0_attn_w_k, L0_attn_w_v, L0_attn_w_o, L0_attn_rel_bias_table, L0_ffn_rw1, L0_ffn_rb1, L0_ffn_rw2, L0_ffn_rb2, L0_ffn_ew1, L0_ffn_eb1, L0_ffn_ew2, L0_ffn_eb2):
    import jax
    import jax.numpy as jnp

    def _L0_xattn_ref(query, key, value, in_proj_weight, in_proj_bias, out_proj_weight, out_proj_bias, lambda_q1, lambda_k1, lambda_q2, lambda_k2):
        import jax, jax.numpy as jnp
        import numpy as np
        import math
        EMBED_DIM = 128
        NUM_HEADS = 16
        HEAD_DIM = EMBED_DIM // NUM_HEADS
        SUB_HEAD_DIM = HEAD_DIM // 2
        SCALING = 1.0 / math.sqrt(SUB_HEAD_DIM)
        LAMBDA_INIT = 0.8 - 0.6 * math.exp(-0.3 * 0)
        B, T, D = query.shape
        S = key.shape[1]
        H, hd, sd = (NUM_HEADS, HEAD_DIM, SUB_HEAD_DIM)
        qw, kw, vw = jnp.split(in_proj_weight, 3, axis=0)
        qb, kb, vb = jnp.split(in_proj_bias, 3, axis=0)
        q = query @ qw.T + qb
        k = key @ kw.T + kb
        v = value @ vw.T + vb
        q = q.reshape(B, T, H, hd).transpose(0, 2, 1, 3)
        k = k.reshape(B, S, H, hd).transpose(0, 2, 1, 3)
        v = v.reshape(B, S, H, hd).transpose(0, 2, 1, 3)
        q1, q2 = (q[..., :sd], q[..., sd:])
        k1, k2 = (k[..., :sd], k[..., sd:])
        logits_1 = jnp.einsum('bhtd,bhsd->bhts', q1, k1) * SCALING
        logits_2 = jnp.einsum('bhtd,bhsd->bhts', q2, k2) * SCALING
        a1 = jax.nn.softmax(logits_1, axis=-1)
        a2 = jax.nn.softmax(logits_2, axis=-1)
        lam = jnp.exp(jnp.dot(lambda_q1, lambda_k1)) - jnp.exp(jnp.dot(lambda_q2, lambda_k2)) + LAMBDA_INIT
        diff_weights = a1 - lam * a2
        attn_output = jnp.einsum('bhts,bhsd->bhtd', diff_weights, v)
        attn_output = attn_output * (1.0 - LAMBDA_INIT)
        attn_output = attn_output.transpose(0, 2, 1, 3).reshape(B, T, D)
        output = attn_output @ out_proj_weight.T + out_proj_bias
        return output

    def _L0_attn_ref(x, w_q, w_k, w_v, w_o, rel_bias_table):
        import jax, jax.numpy as jnp
        import numpy as np
        import math
        D_MODEL = 128
        N_HEADS = 16
        D_K = D_MODEL // N_HEADS
        NUM_BUCKETS = 32
        MAX_DISTANCE = 128
        BIDIRECTIONAL = True

        def _relative_position_bucket(relative_position):
            num_buckets = NUM_BUCKETS
            ret = jnp.zeros_like(relative_position)
            n = -relative_position
            if BIDIRECTIONAL:
                num_buckets //= 2
                ret = ret + (n < 0).astype(jnp.int32) * num_buckets
                n = jnp.abs(n)
            else:
                n = jnp.maximum(n, 0)
            max_exact = num_buckets // 2
            is_small = n < max_exact
            val_if_large = max_exact + (jnp.log(jnp.maximum(n, 1).astype(jnp.float32) / max_exact) / math.log(MAX_DISTANCE / max_exact) * (num_buckets - max_exact)).astype(jnp.int32)
            val_if_large = jnp.minimum(val_if_large, num_buckets - 1)
            return ret + jnp.where(is_small, n, val_if_large)

        def _position_bias(seq_len, rel_bias_table):
            pos = jnp.arange(seq_len, dtype=jnp.int32)
            relative_position = pos[None, :] - pos[:, None]
            buckets = _relative_position_bucket(relative_position)
            values = rel_bias_table[buckets]
            return jnp.transpose(values, (2, 0, 1))
        B, S, _ = x.shape
        q = (x @ w_q.T).reshape(B, S, N_HEADS, D_K)
        k = (x @ w_k.T).reshape(B, S, N_HEADS, D_K)
        v = (x @ w_v.T).reshape(B, S, N_HEADS, D_K)
        scores = jnp.einsum('bqhd,bkhd->bhqk', q, k) / math.sqrt(D_K)
        scores = scores + _position_bias(S, rel_bias_table)[None]
        attn = jax.nn.softmax(scores, axis=-1)
        out = jnp.einsum('bhqk,bkhd->bqhd', attn, v).reshape(B, S, D_MODEL)
        return out @ w_o.T

    def _L0_ffn_ref(x, rw1, rb1, rw2, rb2, ew1, eb1, ew2, eb2):
        import jax, jax.numpy as jnp
        import numpy as np
        B, T, C, E, K, CAP, H = (8, 256, 128, 8, 2, 512, 512)
        Bx, Tx, Cx = x.shape
        N = Bx * Tx
        logits = jax.nn.relu(x @ rw1 + rb1) @ rw2 + rb2
        vals, ids = jax.lax.top_k(logits, K)
        probs = jax.nn.softmax(vals, axis=-1)
        ids_f = ids.reshape(N * K)
        probs_f = probs.reshape(N * K)
        xr = jnp.repeat(x.reshape(N, Cx), K, axis=0)
        m = jax.nn.one_hot(ids_f, E, dtype=jnp.int32)
        pos = jnp.cumsum(m, axis=0) - 1
        pos_tok = jnp.take_along_axis(pos, ids_f[:, None], axis=1)[:, 0]
        keep = (pos_tok < CAP).astype(x.dtype)
        pos_c = jnp.clip(pos_tok, 0, CAP - 1)
        disp = jnp.zeros((E, CAP, Cx), x.dtype).at[ids_f, pos_c].add(xr * keep[:, None])
        h = jax.nn.relu(jnp.einsum('enc,ech->enh', disp, ew1) + eb1[:, None, :])
        eo = jnp.einsum('enh,ehc->enc', h, ew2) + eb2[:, None, :]
        y = eo[ids_f, pos_c] * (probs_f * keep)[:, None]
        return y.reshape(Bx, Tx, K, Cx).sum(axis=2)
    x = x + _L0_xattn_ref(_layernorm(x, axis=-1), ctx_1024, ctx_1024, L0_xattn_in_proj_weight, L0_xattn_in_proj_bias, L0_xattn_out_proj_weight, L0_xattn_out_proj_bias, L0_xattn_lambda_q1, L0_xattn_lambda_k1, L0_xattn_lambda_q2, L0_xattn_lambda_k2)
    x = x + _L0_attn_ref(_layernorm(x, axis=-1), L0_attn_w_q, L0_attn_w_k, L0_attn_w_v, L0_attn_w_o, L0_attn_rel_bias_table)
    x = x + _L0_ffn_ref(_layernorm(x, axis=-1), L0_ffn_rw1, L0_ffn_rb1, L0_ffn_rw2, L0_ffn_rb2, L0_ffn_ew1, L0_ffn_eb1, L0_ffn_ew2, L0_ffn_eb2)
    return x

_drawn_inputs = setup_inputs


def setup_inputs(seed=0):
    import zlib

    import numpy as np

    out = dict(_drawn_inputs(seed))
    spreads = {'L0_xattn_in_proj_bias': (0.0, 0.1),
     'L0_xattn_out_proj_bias': (0.0, 0.1),
     'L0_ffn_rb1': (0.0, 0.286),
     'L0_ffn_rb2': (0.0, 0.1),
     'L0_ffn_eb1': (0.0, 0.421),
     'L0_ffn_eb2': (0.0, 0.1)}
    factors = {'L0_xattn_lambda_q1': 8.0,
     'L0_xattn_lambda_k1': 8.0,
     'L0_xattn_lambda_q2': 5.179,
     'L0_xattn_lambda_k2': 5.179,
     'L0_attn_rel_bias_table': 3.833}
    for name, (base, spread) in spreads.items():
        noise = np.random.default_rng([zlib.crc32(name.encode()), seed]).standard_normal(out[name].shape)
        drawn = base * np.exp(spread * noise) if base else spread * noise
        out[name] = jnp.asarray(drawn.astype(out[name].dtype))
    for name, factor in factors.items():
        out[name] = (out[name] * factor).astype(out[name].dtype)
    return out
```

```python
from contextlib import ExitStack

import numpy as np

import concourse.bass as bass
from concourse import mybir

F32 = mybir.dt.float32
F16 = mybir.dt.float16
U32 = mybir.dt.uint32
ALU = mybir.AluOpType
ACT = mybir.ActivationFunctionType
AX = mybir.AxisListType

P = 128
T = 64
S = 6272
D = 128
H = 16
HD = D // H
SUB = HD // 2
GROUPS = H // 2
GD = 2 * HD
BLK = 32
STK = 4 * GD
CHUNKS = 7
CK = S // CHUNKS
HALF = CK // 2
KT = S // P
TPC = KT // CHUNKS
ENTRY_TILES = [2, 2, 2, 1]
ENTRY0 = [0, 2, 4, 6]
EPC = len(ENTRY_TILES)
COLS = 2 * 2 * T
PER_SLOT = EPC * CHUNKS + 1
MROW = EPC * CHUNKS
RING = 3
PROBS = 8
VW = HD + 1
SCALE_IN = 16.0
MSCALE = SCALE_IN * SCALE_IN
EPS = 1e-5
LAMBDA_INIT = 0.8 - 0.6
E = 8
FH = 512
FC = FH // P
LEAD = 6

A_COLS = dict(x=D, ident=P, bk=1, bq=GROUPS, maskq=4, wk=D, wq=GROUPS * STK)
A_FIRST = A_COLS["x"] + A_COLS["ident"] + 1 + GROUPS + 4
B_COLS = dict(wv=D, sel=2 * VW, vb=D, bo=D, lamq=2 * SUB, lamk=2 * SUB, wo=D, awq=D, awk=D, awv=D, awo=D,
              maskk=H // 2, tri=E * E, pair=T, flip=P)
D_COLS = dict(table=H, onehot=2 * T - 1, blk=FC * P, blk8=E * T, rb1=P, eb1=4 * P, parsel=P, eb2=4 * D, ones=P, rb2=E)


def offsets(cols):
    out, at = {}, 0
    for k, n in cols.items():
        out[k] = (at, at + n)
        at += n
    return out, at


A_AT, A_N = offsets(A_COLS)
B_AT, B_N = offsets(B_COLS)
D_AT, D_N = offsets(D_COLS)


def perceiver_layer(nc, a_in, ctx_in, b_in, ew1_in, ew2_in, rw1_in, rw2_in, d_in, bias_scratch, kparts_dram, out):
    with ExitStack() as ctx:
        def sb(name, shape, dt=F32):
            return ctx.enter_context(nc.sbuf_tensor(name, shape, dt))

        def sem(name):
            return ctx.enter_context(nc.semaphore(name))

        wa = sb("wa", [P, A_N])
        wb = sb("wb", [P, B_N])
        wd = sb("wd", [32, D_N])
        ctxT = sb("ctxT", [P, S])
        kparts = sb("kparts", [P, 2, S], F16)
        kst = sb("kst", [P, 2, S], F16)
        qs = sb("qs", [P, GROUPS, COLS], F16)
        vall = sb("vall", [P, GROUPS, KT, 2 * VW])
        vcur = sb("vcur", [P, 2, KT, 2 * VW])
        probs = sb("probs", [P, PROBS, 2 * COLS])
        accs = sb("accs", [P, GROUPS, COLS])
        ew1 = kparts[:, :, :].rearrange("p a n -> p (a n)").bitcast(F32)[:, 0:E * FH]
        ew2 = ctxT[:, 0:E * FC * D]
        rw1 = sb("rw1", [P, FH])
        rw2 = sb("rw2", [P, FC * E])
        ident16 = sb("ident16", [P, P], F16)
        wk16 = sb("wk16", [P, D])
        bk16 = sb("bk16", [P, 1])
        stats = sb("stats", [T, 6])
        mv = sb("mv", [T, 2])
        rstd = sb("rstd", [T, 1])
        veps = sb("veps", [T, 1])
        power = sb("power", [T, 1])
        xn = sb("xn", [T, D])
        xnT = sb("xnT", [P, T])
        bq16 = sb("bq16", [STK, GROUPS])
        qf = sb("qf", [STK, GROUPS, T])
        qparts = sb("qparts", [STK, GROUPS, T], F16)
        mx = sb("mx", [P, 2, 2, CHUNKS])
        negmax = sb("negmax", [P, 2])
        negmax16 = sb("negmax16", [P, 2, 2], F16)
        lamp = sb("lamp", [T, 2, SUB])
        lamd = sb("lamd", [T, 2])
        lame = sb("lame", [T, 2])
        lamx = sb("lamx", [T, 1])
        spare = sb("spare", [1, 1])
        coef = sb("coef", [T, 2])
        vsc = sb("vsc", [T, 1])
        vbt = sb("vbt", [T, D])
        xbo = sb("xbo", [T, D])
        rec = sb("rec", [T, H, 2])
        o4 = sb("o4", [T, H, 2, HD])
        osum = sb("osum", [T, D])
        attn = sb("attn", [T, D])
        attnT = sb("attnT", [P, T])
        x1 = sb("x1", [T, D])
        x1T = sb("x1T", [P, 2, T])
        qTs = sb("qTs", [P, T])
        kbd = sb("kbd", [P, H // 2, T])
        vbd = sb("vbd", [P, H // 2, 2, VW])
        relT = sb("relT", [H, 2 * T - 1])
        relb = sb("relb", [P, H // 2, T])
        smx = sb("smx", [P, H // 2])
        ssub = sb("ssub", [P, H // 2, T])
        sexp = sb("sexp", [P, H // 2, T])
        pT = sb("pT", [P, 4, 2, T])
        rec2 = sb("rec2", [T, H])
        attn2 = sb("attn2", [T, D])
        attn2T = sb("attn2T", [P, T])
        x2 = sb("x2", [T, D])
        x2T = sb("x2T", [P, 2, T])
        hr = sb("hr", [P, FC, P])
        lg = sb("lg", [P, E])
        gt = sb("gt", [P, E, E])
        eq = sb("eq", [P, E, E])
        eqt = sb("eqt", [P, E, E])
        ahead = sb("ahead", [P, E, E])
        rank = sb("rank", [P, E])
        lmx = sb("lmx", [P, 1])
        lsub = sb("lsub", [P, E])
        lexp = sb("lexp", [P, E])
        sel2 = sb("sel2", [P, E])
        den = sb("den", [P, 1])
        rden = sb("rden", [P, 1])
        gate = sb("gate", [P, 4])
        hs = sb("hs", [P, 4, 8 * T])
        gated = sb("gated", [P, 4, D])
        y = sb("y", [T, D])

        def a_(k):
            return wa[:, A_AT[k][0]:A_AT[k][1]]

        def b_(k, n=P):
            return wb[0:n, B_AT[k][0]:B_AT[k][1]]

        def d_(k, n):
            return wd[0:n, D_AT[k][0]:D_AT[k][1]]

        ident = a_("ident")

        p1 = ctx.enter_context(nc.psum_tensor("p1", [P, 2, 2, 512], F32))
        ring = ctx.enter_context(nc.psum_tensor("ring", [P, RING, 512], F32))
        acc = ctx.enter_context(nc.psum_tensor("acc", [P, 512], F32))

        a_in_s = sem("a_loaded")
        b_in_s = sem("b_loaded")
        d_in_s = sem("d_loaded")
        ffn_in = sem("ffn_weights_loaded")
        ctx_in_s = [sem(f"ctx_loaded{c}") for c in range(CHUNKS)]
        kst_in = [[sem(f"keys_stacked{p}_{c}") for c in range(CHUNKS)] for p in range(2)]
        k_out = [sem(f"keys_spread{c}") for c in range(CHUNKS)]
        wk_in = sem("wk_loaded")
        wq_in = sem("wq_loaded")
        v_in = [sem(f"values_in{p}") for p in range(2)]
        qs_zero = sem("qs_zeroed")
        kst_zero = sem("kst_zeroed")
        kst_set = sem("kst_row_set")
        ones_set = sem("ones_set")
        ln_s = sem("ln_steps")
        veps_done = sem("variance_with_eps")
        power_set = sem("power_set")
        xn_done = sem("xn_done")
        xnT_ps = sem("xnT_in_psum")
        xnT_done = sem("xnT_done")
        q_ps = sem("q_in_psum")
        id16_done = sem("ident16_done")
        wk_done = sem("wk_scaled")
        q_read = sem("q_out_of_psum")
        qsplit = sem("q_split_steps")
        q0_done = sem("queries0_done")
        q_done = sem("queries_done")
        klo_done = sem("klo_done")
        p1_full = sem("pass1_full")
        p1_empty = sem("pass1_reduced")
        nm_raw = sem("negmax_done")
        m_ready = sem("negmax16_ready")
        lg_full = sem("logits_full")
        act_done = sem("ring_entry_read")
        probs_free = sem("probs_free")
        acc_free = sem("sums_bank_free")
        lam_s = sem("lambda_steps")
        lam_e = sem("lambda_exp")
        coef_done = sem("coef_done")
        vbt_done = sem("vbt_done")
        xbo_done = sem("xbo_done")
        vbd_zero = sem("vbd_zeroed")
        vbd_ones = sem("vbd_ones_set")
        po_ps = sem("attention_sums_in_psum")
        norm_s = sem("normalise_steps")
        attn_done = sem("attn_done")
        attnT_ps = sem("attnT_in_psum")
        attnT_done = sem("attnT_done")
        proj1_ps = sem("cross_attention_in_psum")
        x1_done = sem("x1_done")
        qk_ps = sem("self_qk_in_psum")
        v_ps = sem("self_v_in_psum")
        qk_done = sem("self_qk_done")
        vbd_done = sem("self_v_done")
        sc_ps = sem("self_scores_in_psum")
        smx_done = sem("self_max_done")
        ssub_done = sem("self_shifted")
        sexp_done = sem("self_exp_done")
        pT_ps = sem("self_probsT_in_psum")
        pT_done = sem("self_probsT_done")
        pv_ps = sem("self_values_in_psum")
        rec2_done = sem("self_reciprocal_done")
        attn2_done = sem("self_attn_done")
        attn2T_ps = sem("self_attnT_in_psum")
        attn2T_done = sem("self_attnT_done")
        proj2_ps = sem("self_attention_in_psum")
        x2_done = sem("x2_done")
        hr_ps = sem("router_hidden_in_psum")
        hr_done = sem("router_hidden_done")
        lg_ps = sem("router_logits_in_psum")
        gate_s = sem("gate_steps")
        lexp_done = sem("router_exp_done")
        gate_done = sem("gates_done")
        he_ps = sem("expert_hidden_in_psum")
        hs_done = sem("expert_hidden_done")
        eo_ps = sem("expert_out_in_psum")
        gated_done = sem("gated_done")
        y_ps = sem("mixture_in_psum")
        y_done = sem("y_done")
        out_done = sem("out_written")
        rel_ps = sem("rel_in_psum")
        rel_sb = sem("rel_in_sbuf")
        rel_out = sem("rel_in_dram")
        rel_in = sem("rel_spread")

        block = ctx.enter_context(nc.Block())

        def chunk_no(g, c, h):
            return 2 * CHUNKS * g + 2 * c + h

        def entry_no(g, c, e):
            return PER_SLOT * (g + 1) + EPC * c + e

        def products_done(g):
            return PROBS + EPC * CHUNKS * (g + 1)

        def stacked(it, par, ahead_by):
            return (it + (par + ahead_by) // 2 + 1) * 16

        def bank(i):
            return p1[:, i // 2, i % 2, :] if i < 4 else ring[:, i - 4, :] if i < 7 else acc[:, :]

        po = bank(4)[0:T, 0:2 * H * VW].rearrange("p (h s v) -> p h s v", h=H, s=2)
        pv = bank(4)[0:T, 0:H * VW].rearrange("p (h v) -> p h v", h=H)
        sc = bank(6).rearrange("p (h k) -> p h k", h=H // 2)
        ALL_READ = PER_SLOT * (GROUPS + 1) - 1

        def expert_bias(pe):
            pe.wait_ge(p1_empty, chunk_no(GROUPS, 0, 0))
            for b in range(4):
                pe.matmul(bank(b), d_("eb1", 8)[:, P * b:P * b + P], d_("blk8", 8), start=True, stop=False,
                          skip_group_check=True)

        def tail_pe(pe):
            pe.wait_ge(act_done, ALL_READ)
            for g in range(GROUPS):
                if g in (0, GROUPS - 1):
                    pe.wait_ge(acc_free, GROUPS + (g > 0))
                for h in range(2):
                    for s in range(2):
                        i = (2 * g + h) * 2 + s
                        k = T * (2 * h + s)
                        last = pe.matmul(bank(4)[0:T, VW * i:VW * i + VW], accs[:, g, k:k + T],
                                         b_("sel")[:, VW * h:VW * h + VW], start=True, stop=True)
            last.then_inc(po_ps, 1)
            pe.wait_ge(rel_in, 32)
            pe.matmul(bank(6), b_("flip"), relb[:, :, :].rearrange("p h k -> p (h k)"), start=True, stop=False,
                      skip_group_check=True)
            pe.wait_ge(attn_done, 1)
            pe.transpose(bank(5)[:, 0:T], attn[:, :], ident[0:T, 0:T]).then_inc(attnT_ps, 1)
            pe.wait_ge(attnT_done, 1)
            pe.matmul(bank(7)[0:T, 0:D], attnT[:, :], b_("wo"), start=True, stop=True).then_inc(proj1_ps, 1)
            pe.wait_ge(xn_done, 2)
            pe.transpose(bank(5)[:, 0:T], xn[:, :], ident[0:T, 0:T]).then_inc(xnT_ps, 1)
            pe.wait_ge(xnT_done, 2)
            pe.matmul(bank(4)[:, 0:T], b_("awq"), x1T[:, 0, :], start=True, stop=True)
            pe.matmul(bank(4)[:, T:2 * T], b_("awk"), x1T[:, 0, :], start=True, stop=True).then_inc(qk_ps, 1)
            pe.wait_ge(x1_done, 1)
            pe.matmul(bank(7)[:, 0:D], x1T[:, :, :].rearrange("p a t -> p (a t)"), b_("awv"),
                      start=True, stop=True).then_inc(v_ps, 1)
            pe.wait_ge(qk_done, 2)
            for half in range(2):
                r = T * half
                last = pe.matmul(bank(6)[r:r + T, :], qTs[r:r + T, :],
                                 kbd[r:r + T, :, :].rearrange("p h k -> p (h k)"), start=False, stop=True,
                                 skip_group_check=True)
            last.then_inc(sc_ps, 1)
            pe.wait_ge(sexp_done, 1)
            pe.wait_ge(vbd_done, 2)
            for n in range(4):
                last = pe.transpose(bank(5 + 2 * (n // 2))[:, P * (n % 2):P * (n % 2) + P],
                                    sexp[:, 2 * n:2 * n + 2, :].rearrange("p h k -> p (h k)"), ident)
            last.then_inc(pT_ps, 1)
            pe.wait_ge(d_in_s, 16)
            pe.matmul(bank(6), d_("rb1", FC), d_("blk", FC), start=True, stop=False, skip_group_check=True)
            pe.wait_ge(pT_done, 2)
            for n in range(H // 2):
                last = pe.matmul(bank(4)[0:T, 2 * VW * n:2 * VW * n + 2 * VW], pT[:, n % 4, n // 4, :],
                                 vbd[:, n, :, :].rearrange("p a v -> p (a v)"), start=True, stop=True)
            last.then_inc(pv_ps, 1)
            pe.matmul(bank(7), d_("parsel", 2), d_("eb2", 2), start=True, stop=False, skip_group_check=True)
            pe.wait_ge(attn2_done, 1)
            pe.transpose(bank(5)[:, 0:T], attn2[:, :], ident[0:T, 0:T]).then_inc(attn2T_ps, 1)
            pe.wait_ge(attn2T_done, 1)
            pe.matmul(bank(4)[0:T, 0:D], attn2T[:, :], b_("awo"), start=True, stop=True).then_inc(proj2_ps, 1)
            pe.wait_ge(xn_done, 3)
            pe.transpose(bank(5)[:, 0:T], xn[:, :], ident[0:T, 0:T]).then_inc(xnT_ps, 1)
            pe.wait_ge(ffn_in, 64)
            pe.wait_ge(xnT_done, 3)
            x2all = x2T[:, :, :].rearrange("p a t -> p (a t)")
            for f in range(FC):
                last = pe.matmul(bank(6)[:, P * f:P * f + P], rw1[:, P * f:P * f + P], x2all,
                                 start=False, stop=True, skip_group_check=True)
            last.then_inc(hr_ps, 1)
            for b in range(4):
                for n in range(8):
                    w = (8 * b + n) * P
                    last = pe.matmul(bank(b)[:, T * n:T * n + T], ew1[:, w:w + P], x2T[:, 0, :],
                                     start=False, stop=True, skip_group_check=True)
                last.then_inc(he_ps, 1)
                if b == 0:
                    pe.wait_ge(hr_done, 1)
                    pe.matmul(bank(5)[:, 0:E], d_("ones", 1), d_("rb2", 1), start=True, stop=False)
                    for f in range(FC):
                        last = pe.matmul(bank(5)[:, 0:E], hr[:, f, :], rw2[:, E * f:E * f + E],
                                         start=False, stop=(f == FC - 1))
                    last.then_inc(lg_ps, 1)
            for b in range(4):
                pe.wait_ge(hs_done, b + 1)
                for f in range(FC):
                    for e2 in range(2):
                        w = ((2 * b + e2) * FC + f) * D
                        last = pe.matmul(bank(7)[T * e2:T * e2 + T, D * b:D * b + D],
                                         hs[:, b, T * (FC * e2 + f):T * (FC * e2 + f) + T], ew2[:, w:w + D],
                                         start=False, stop=True, skip_group_check=True)
            last.then_inc(eo_ps, 1)
            pe.wait_ge(gated_done, 1)
            for b in range(4):
                last = pe.matmul(bank(4)[0:T, 0:D], b_("pair"), gated[:, b, :], start=(b == 0), stop=(b == 3))
            last.then_inc(y_ps, 1)

        def tail_act(act):
            act.wait_ge(vbd_ones, 2)
            act.wait_ge(v_ps, 1)
            for h2 in range(2):
                r = T * h2
                nc.scalar.copy(vbd[r:r + T, :, h2, 0:HD],
                               bank(7)[r:r + T, 0:D].rearrange("p (n h v) -> p n h v", h=2, v=HD)[:, :, h2, :]
                               ).then_inc(vbd_done, 1)
            act.wait_ge(ssub_done, 1)
            nc.scalar.activation(sexp[:, :, :], ssub[:, :, :], ACT.Exp).then_inc(sexp_done, 1)
            act.wait_ge(pT_ps, 1)
            nc.scalar.copy(pT[:, 2:4, :, :].rearrange("p a b t -> p (a b t)"), bank(7)[:, 0:2 * P]).then_inc(pT_done, 1)
            act.wait_ge(hr_ps, 1)
            nc.scalar.activation(hr[:, :, :].rearrange("p f t -> p (f t)"), bank(6), ACT.Relu).then_inc(hr_done, 1)
            for b in range(4):
                act.wait_ge(he_ps, b + 1)
                nc.scalar.activation(hs[:, b, :], bank(b), ACT.Relu).then_inc(hs_done, 1)
                if b == 1:
                    act.wait_ge(gate_s, 3)
                    nc.scalar.activation(lexp[:, :], lsub[:, :], ACT.Exp).then_inc(lexp_done, 1)

        def deviation(pool, n):
            pool.wait_ge(ln_s, 3 * n + 2)
            nc.gpsimd.tensor_scalar(veps[:, :], mv[:, 1:2], EPS, None, ALU.add).then_inc(veps_done, 1)
            pool.wait_ge(veps_done, n + 1)
            nc.gpsimd.tensor_tensor(rstd[:, :], veps[:, :], power[:, :], ALU.pow).then_inc(ln_s, 1)

        def layer_norm(dve, x, n):
            nc.vector.bn_stats(stats[:, :], x).then_inc(ln_s, 1)
            dve.wait_ge(ln_s, 3 * n + 1)
            nc.vector.bn_aggr(mv[:, :], stats[:, :]).then_inc(ln_s, 1)
            dve.wait_ge(ln_s, 3 * n + 3)
            nc.vector.tensor_scalar(xn[:, :], x, mv[:, 0:1], rstd[:, 0:1],
                                    ALU.subtract, ALU.mult).then_inc(xn_done, 1)

        def tail_dve(dve):
            dve.wait_ge(po_ps, 1)
            nc.vector.reciprocal(rec[:, :, :], po[:, :, :, HD]).then_inc(norm_s, 1)
            dve.wait_ge(norm_s, 1)
            nc.vector.tensor_tensor(rec[:, :, :], rec[:, :, :], coef[:, :].unsqueeze(1).to_broadcast([T, H, 2]),
                                    ALU.mult).then_inc(norm_s, 1)
            dve.wait_ge(norm_s, 2)
            nc.vector.tensor_tensor(o4[:, :, :, :], po[:, :, :, 0:HD],
                                    rec[:, :, :].unsqueeze(3).to_broadcast([T, H, 2, HD]), ALU.mult).then_inc(norm_s, 1)
            dve.wait_ge(norm_s, 3)
            nc.vector.tensor_tensor(osum[:, :].rearrange("p (h v) -> p h v", h=H), o4[:, :, 0, :], o4[:, :, 1, :],
                                    ALU.add).then_inc(norm_s, 1)
            dve.wait_ge(norm_s, 4)
            nc.vector.tensor_tensor(attn[:, :], osum[:, :], vbt[:, :], ALU.add).then_inc(attn_done, 1)
            dve.wait_ge(attnT_ps, 1)
            nc.vector.tensor_copy(attnT[:, :], bank(5)[:, 0:T]).then_inc(attnT_done, 1)
            dve.wait_ge(proj1_ps, 1)
            nc.vector.tensor_tensor(x1[:, :], bank(7)[0:T, 0:D], xbo[:, :], ALU.add).then_inc(x1_done, 1)
            dve.wait_ge(x1_done, 1)
            layer_norm(dve, x1[:, :], 1)
            dve.wait_ge(xnT_ps, 2)
            nc.vector.tensor_copy(x1T[:, :, :], bank(5)[:, 0:T].unsqueeze(1).to_broadcast([P, 2, T])).then_inc(xnT_done, 1)
            dve.wait_ge(qk_ps, 1)
            nc.vector.tensor_scalar(qTs[:, :], bank(4)[:, 0:T], HD ** -0.5, None, ALU.mult).then_inc(qk_done, 1)
            nc.vector.tensor_tensor(kbd[:, :, :], bank(4)[:, T:2 * T].unsqueeze(1).to_broadcast([P, H // 2, T]),
                                    b_("maskk").unsqueeze(2).to_broadcast([P, H // 2, T]), ALU.mult).then_inc(qk_done, 1)
            dve.wait_ge(sc_ps, 1)
            nc.vector.tensor_reduce(smx[:, :], sc, AX.X, ALU.max).then_inc(smx_done, 1)
            dve.wait_ge(smx_done, 1)
            nc.vector.tensor_tensor(ssub[:, :, :], sc, smx[:, :].unsqueeze(2).to_broadcast([P, H // 2, T]),
                                    ALU.subtract).then_inc(ssub_done, 1)
            dve.wait_ge(pT_ps, 1)
            nc.vector.tensor_copy(pT[:, 0:2, :, :].rearrange("p a b t -> p (a b t)"), bank(5)[:, 0:2 * P]).then_inc(pT_done, 1)
            dve.wait_ge(pv_ps, 1)
            nc.vector.reciprocal(rec2[:, :], pv[:, :, HD]).then_inc(rec2_done, 1)
            dve.wait_ge(rec2_done, 1)
            nc.vector.tensor_tensor(attn2[:, :].rearrange("p (h v) -> p h v", h=H), pv[:, :, 0:HD],
                                    rec2[:, :].unsqueeze(2).to_broadcast([T, H, HD]), ALU.mult).then_inc(attn2_done, 1)
            dve.wait_ge(attn2T_ps, 1)
            nc.vector.tensor_copy(attn2T[:, :], bank(5)[:, 0:T]).then_inc(attn2T_done, 1)
            dve.wait_ge(proj2_ps, 1)
            nc.vector.tensor_tensor(x2[:, :], bank(4)[0:T, 0:D], x1[:, :], ALU.add).then_inc(x2_done, 1)
            dve.wait_ge(x2_done, 1)
            layer_norm(dve, x2[:, :], 2)
            dve.wait_ge(xnT_ps, 3)
            nc.vector.tensor_copy(x2T[:, :, :], bank(5)[:, 0:T].unsqueeze(1).to_broadcast([P, 2, T])).then_inc(xnT_done, 1)
            dve.wait_ge(lg_ps, 1)
            nc.vector.tensor_copy(lg[:, :], bank(5)[:, 0:E]).then_inc(gate_s, 1)
            dve.wait_ge(gate_s, 1)
            nc.vector.tensor_reduce(lmx[:, :], lg[:, :], AX.X, ALU.max).then_inc(gate_s, 1)
            dve.wait_ge(gate_s, 2)
            nc.vector.tensor_scalar(lsub[:, :], lg[:, :], lmx[:, 0:1], None, ALU.subtract).then_inc(gate_s, 1)
            other = lg[:, :].unsqueeze(1).to_broadcast([P, E, E])
            own = lg[:, :].unsqueeze(2).to_broadcast([P, E, E])
            nc.vector.tensor_tensor(gt[:, :, :], other, own, ALU.is_gt).then_inc(gate_s, 1)
            nc.vector.tensor_tensor(eq[:, :, :], other, own, ALU.is_equal).then_inc(gate_s, 1)
            dve.wait_ge(gate_s, 5)
            nc.vector.tensor_tensor(eqt[:, :, :].rearrange("p a b -> p (a b)"), eq[:, :, :].rearrange("p a b -> p (a b)"),
                                    b_("tri"), ALU.mult).then_inc(gate_s, 1)
            dve.wait_ge(gate_s, 6)
            nc.vector.tensor_tensor(ahead[:, :, :], gt[:, :, :], eqt[:, :, :], ALU.add).then_inc(gate_s, 1)
            dve.wait_ge(gate_s, 7)
            nc.vector.tensor_reduce(rank[:, :], ahead[:, :, :], AX.X, ALU.add).then_inc(gate_s, 1)
            dve.wait_ge(gate_s, 8)
            dve.wait_ge(lexp_done, 1)
            nc.vector.scalar_tensor_tensor(out=sel2[:, :], in0=rank[:, :], scalar=2.0, in1=lexp[:, :],
                                           op0=ALU.is_lt, op1=ALU.mult).then_inc(gate_s, 1)
            dve.wait_ge(gate_s, 9)
            nc.vector.tensor_reduce(den[:, :], sel2[:, :], AX.X, ALU.add).then_inc(gate_s, 1)
            dve.wait_ge(gate_s, 10)
            nc.vector.reciprocal(rden[:, :], den[:, :]).then_inc(gate_s, 1)
            dve.wait_ge(gate_s, 11)
            for e2 in range(2):
                r = T * e2
                nc.vector.tensor_scalar(gate[r:r + T, :], sel2[r:r + T, :].rearrange("p (b a) -> p b a", a=2)[:, :, e2],
                                        rden[r:r + T, 0:1], None, ALU.mult).then_inc(gate_done, 1)
            dve.wait_ge(gate_done, 2)
            dve.wait_ge(eo_ps, 1)
            nc.vector.tensor_tensor(gated[:, :, :], bank(7).rearrange("p (b d) -> p b d", b=4),
                                    gate[:, :].unsqueeze(2).to_broadcast([P, 4, D]), ALU.mult).then_inc(gated_done, 1)
            dve.wait_ge(y_ps, 1)
            nc.vector.tensor_tensor(y[:, :], bank(4)[0:T, 0:D], x2[:, :], ALU.add).then_inc(y_done, 1)

        @block.sync
        def _(sp):
            def spread_keys(c):
                sp.dma_start(kparts_dram[:, :, CK * c:CK * c + CK],
                             kparts[:, :, CK * c:CK * c + CK]).then_inc(k_out[c], 16)

            def stack_keys(g, c, par):
                k = kparts_dram[GD * g:GD * g + GD, :, CK * c:CK * c + CK]
                src = bass.AP(k.tensor, k.offset, [[0, 2], [S, 2 * GD], [1, CK]])
                sp.dma_start(kst[0:STK, par, CK * c:CK * c + CK], src).then_inc(kst_in[par][c], 16)

            for s0, s1, s in ((0, A_FIRST, a_in_s), (A_FIRST, A_FIRST + D, wk_in), (A_FIRST + D, A_N, wq_in)):
                sp.dma_start(wa[:, s0:s1], a_in[:, s0:s1]).then_inc(s, 16)
            for c in range(CHUNKS):
                sp.wait_ge(klo_done, 2 * c + 2)
                spread_keys(c)
                sp.wait_ge(k_out[c], 16)
                stack_keys(0, c, 0)
            for c in range(CHUNKS):
                stack_keys(1, c, 1)
            sp.wait_ge(act_done, 28)
            for g in range(2):
                sp.dma_start(vcur[:, g, :, :], vall[:, g, :, :]).then_inc(v_in[g], 16)
            sp.wait_ge(rel_sb, 1)
            sp.dma_start(bias_scratch, relT[:, :]).then_inc(rel_out, 16)
            sp.wait_ge(rel_out, 16)
            n = 2 * T - 1
            for half in range(2):
                src = bass.AP(bias_scratch.tensor, bias_scratch.offset + half * (H // 2) * n,
                              [[1, T], [n, H // 2], [1, T]])
                sp.dma_start(relb[T * half:T * half + T, :, :], src).then_inc(rel_in, 16)
            for g in range(GROUPS - 2):
                for c in range(CHUNKS):
                    sp.wait_ge(lg_full, entry_no(g, c, EPC))
                    stack_keys(g + 2, c, g % 2)
                sp.wait_ge(probs_free, products_done(g))
                sp.dma_start(vcur[:, g % 2, :, :], vall[:, g + 2, :, :]).then_inc(v_in[g % 2], 16)
            sp.wait_ge(y_done, 1)
            sp.dma_start(out, y[:, :]).then_inc(out_done, 16)
            sp.wait_ge(out_done, 16)

        @block.gpsimd
        def _(pool):
            nc.gpsimd.memset(power[:, :], -0.5).then_inc(power_set, 1)
            nc.gpsimd.memset(qs[STK:P, :, :].rearrange("p g n -> p (g n)").bitcast(U32), 0).then_inc(qs_zero, 1)
            pool.wait_ge(power_set, 1)
            deviation(pool, 0)
            nc.gpsimd.memset(kst[STK:P, 1, :].bitcast(U32), 0).then_inc(kst_zero, 1)
            pool.wait_ge(kst_zero, 2)
            for n in range(2):
                nc.gpsimd.memset(kst[STK:STK + 1, n, :], MSCALE).then_inc(kst_set, 1)
            pool.wait_ge(kst_set, 2)
            pool.wait_ge(qsplit, 3)
            nc.gpsimd.tensor_tensor(
                qs[0:STK, 1:GROUPS, :].rearrange("p g (a t) -> p g a t", a=4),
                qparts[:, 1:GROUPS, :].unsqueeze(2).to_broadcast([STK, GROUPS - 1, 4, T]),
                a_("maskq")[0:STK, :].unsqueeze(1).unsqueeze(3).to_broadcast([STK, GROUPS - 1, 4, T]),
                ALU.mult).then_inc(q_done, 1)
            nc.gpsimd.memset(vall[:, :, :, :].rearrange("p g t v -> p (g t v)"), 1.0).then_inc(ones_set, 1)
            nc.gpsimd.memset(vbd[:, :, :, :].rearrange("p a b v -> p (a b v)"), 0.0).then_inc(vbd_zero, 1)
            pool.wait_ge(vbd_zero, 1)
            for h2 in range(2):
                nc.gpsimd.memset(vbd[T * h2:T * h2 + T, :, h2, HD:VW], 1.0).then_inc(vbd_ones, 1)
            nc.gpsimd.memset(spare[:, :], 0.0).then_inc(probs_free, PROBS)
            for n in (1, 2):
                deviation(pool, n)

        @block.scalar
        def _(act):
            for c in range(CHUNKS):
                act.dma_start(ctxT[:, CK * c:CK * c + CK], ctx_in[:, CK * c:CK * c + CK]).then_inc(ctx_in_s[c], 16)
            act.dma_start(wb[:, :], b_in).then_inc(b_in_s, 16)
            act.dma_start(wd[:, :], d_in).then_inc(d_in_s, 16)
            act.wait_ge(wk_done, 2)
            for u in range(2 * CHUNKS):
                act.wait_ge(lg_full, u + 1)
                nc.scalar.activation(kparts[:, 0, HALF * u:HALF * u + HALF], ring[:, u % RING, 0:HALF],
                                     ACT.Identity, bias=bk16[:, :]).then_inc(act_done, 1)
            act.wait_ge(ones_set, 1)
            for c in range(CHUNKS):
                for j, (t0, nt) in enumerate(((0, 4), (4, 3))):
                    i = 2 * CHUNKS + 2 * c + j
                    act.wait_ge(lg_full, i + 1)
                    for t in range(nt):
                        last = nc.scalar.copy(
                            vall[:, :, TPC * c + t0 + t, :].rearrange("p g (h v) -> p g h v", v=VW)[:, :, :, 0:HD],
                            ring[:, i % RING, P * t:P * t + P].rearrange("p (g h v) -> p g h v", g=GROUPS, v=HD))
                    last.then_inc(act_done, 1)
            for c in range(CHUNKS):
                act.wait_ge(k_out[c], 16)
            for dst, src in ((ew1, ew1_in), (ew2, ew2_in), (rw1, rw1_in), (rw2, rw2_in)):
                act.dma_start(dst[:, :], src).then_inc(ffn_in, 16)

            def max_row(g):
                act.wait_ge(lg_full, entry_no(g - 1, CHUNKS, 1))
                nc.scalar.copy(qs[STK:STK + 1, bass.ds(g, 1), :].rearrange("p g n -> p (g n)"),
                               ring[0:1, MROW % RING, 0:COLS]).then_inc(act_done, 1)

            def slot(g, par, last):
                for c in range(CHUNKS):
                    for e in range(EPC):
                        k = EPC * c + e
                        n = COLS * ENTRY_TILES[e]
                        act.wait_ge(lg_full, entry_no(g, c, e + 1))
                        act.wait_ge(probs_free, EPC * CHUNKS * g + k + 1)
                        nc.scalar.activation(probs[:, (EPC * CHUNKS * par + k) % PROBS, 0:n],
                                             ring[:, k % RING, 0:n], ACT.Exp,
                                             scale=SUB ** -0.5 / MSCALE).then_inc(act_done, 1)
                if not last:
                    max_row(g + 1)

            act.wait_ge(q_done, 1)
            max_row(0)
            with act.Fori(0, (GROUPS - 2) // 2) as it:
                for par in range(2):
                    slot(2 * it + par, par, False)
            slot(GROUPS - 2, 0, False)
            act.wait_ge(lam_s, 2)
            nc.scalar.activation(lame[:, :], lamd[:, :], ACT.Exp).then_inc(lam_e, 1)
            slot(GROUPS - 1, 1, True)
            tail_act(act)

        @block.vector
        def _(dve):
            nc.vector.memset(kst[STK:P, 0, :].bitcast(U32), 0).then_inc(kst_zero, 1)
            nc.vector.memset(acc[:, 0:COLS], 0.0).then_inc(acc_free, 1)
            dve.wait_ge(a_in_s, 16)
            nc.vector.bn_stats(stats[:, :], a_("x")[0:T, :]).then_inc(ln_s, 1)
            nc.vector.tensor_scalar(bk16[:, :], a_("bk"), SCALE_IN, None, ALU.mult).then_inc(wk_done, 1)
            dve.wait_ge(ln_s, 1)
            nc.vector.bn_aggr(mv[:, :], stats[:, :]).then_inc(ln_s, 1)
            dve.wait_ge(wk_in, 16)
            nc.vector.tensor_scalar(wk16[:, :], a_("wk"), SCALE_IN, None, ALU.mult).then_inc(wk_done, 1)
            nc.vector.tensor_scalar(bq16[:, :], a_("bq")[0:STK, :], SCALE_IN, None, ALU.mult).then_inc(qsplit, 1)
            nc.vector.tensor_copy(ident16[:, :], ident).then_inc(id16_done, 1)
            dve.wait_ge(ln_s, 3)
            nc.vector.tensor_scalar(xn[:, :], a_("x")[0:T, :], mv[:, 0:1], rstd[:, 0:1],
                                    ALU.subtract, ALU.mult).then_inc(xn_done, 1)

            def queries():
                half = slice(STK // 2, STK)
                dve.wait_ge(q_ps, 1)
                dve.wait_ge(qsplit, 1)
                nc.vector.scalar_tensor_tensor(
                    out=qf[:, :, :], in0=p1[0:STK, 0, 1, :].rearrange("p (g t) -> p g t", g=GROUPS), scalar=SCALE_IN,
                    in1=bq16[:, :].unsqueeze(2).to_broadcast([STK, GROUPS, T]),
                    op0=ALU.mult, op1=ALU.add).then_inc(q_read, 1)
                dve.wait_ge(q_read, 1)
                nc.vector.tensor_copy(qparts[:, :, :], qf[:, :, :]).then_inc(qsplit, 1)
                dve.wait_ge(qsplit, 2)
                nc.vector.tensor_tensor(qparts[half, :, :], qf[half, :, :], qparts[half, :, :],
                                        ALU.subtract).then_inc(qsplit, 1)
                dve.wait_ge(qsplit, 3)
                nc.vector.tensor_tensor(
                    qs[0:STK, 0, :].rearrange("p (a t) -> p a t", a=4),
                    qparts[:, 0, :].unsqueeze(1).to_broadcast([STK, 4, T]),
                    a_("maskq")[0:STK, :].unsqueeze(2).to_broadcast([STK, 4, T]), ALU.mult).then_inc(q0_done, 1)

            def low_keys(u):
                dve.wait_ge(act_done, u + 1)
                nc.vector.scalar_tensor_tensor(
                    out=kparts[:, 1, HALF * u:HALF * u + HALF], in0=ring[:, u % RING, 0:HALF], scalar=bk16[:, 0:1],
                    in1=kparts[:, 0, HALF * u:HALF * u + HALF], op0=ALU.add, op1=ALU.subtract).then_inc(klo_done, 1)

            def chunk_max(g, c, h, par):
                dve.wait_ge(p1_full, chunk_no(g, c, h) + 1)
                nc.vector.tensor_reduce(mx[:, par, h, c:c + 1], p1[:, h, :, 0:HALF], AX.XY,
                                        ALU.max).then_inc(p1_empty, 1)

            def group_max(g, par):
                dve.wait_ge(p1_empty, chunk_no(g, CHUNKS, 0))
                nc.vector.tensor_reduce(negmax[:, :], mx[:, par, :, :], AX.X, ALU.max,
                                        negate=True).then_inc(nm_raw, 1)
                dve.wait_ge(nm_raw, g + 1)
                nc.vector.tensor_scalar(negmax16[:, par, :], negmax[:, :], 1.0 / MSCALE, None,
                                        ALU.mult).then_inc(m_ready, 1)

            def save_sums(g):
                dve.wait_ge(probs_free, products_done(g))
                nc.vector.tensor_copy(accs[:, bass.ds(g, 1), :].rearrange("p g n -> p (g n)"),
                                      acc[:, 0:COLS]).then_inc(acc_free, 1)

            for u in range(2):
                low_keys(u)
            dve.wait_ge(xnT_ps, 1)
            nc.vector.tensor_copy(xnT[:, :], p1[:, 0, 0, 0:T]).then_inc(xnT_done, 1)
            for u in range(2, 4):
                low_keys(u)
            queries()
            for u in range(4, LEAD):
                low_keys(u)
            for c in range(CHUNKS):
                for h in range(2):
                    chunk_max(0, c, h, 0)
                    if 2 * c + h + LEAD < 2 * CHUNKS:
                        low_keys(2 * c + h + LEAD)
            group_max(0, 0)
            for h in range(2):
                chunk_max(1, 0, h, 1)
            dve.wait_ge(rel_ps, 1)
            nc.vector.tensor_copy(relT[:, :], acc[0:H, COLS:COLS + 2 * T - 1]).then_inc(rel_sb, 1)

            def lambda_dots():
                dve.wait_ge(b_in_s, 16)
                nc.vector.tensor_tensor(lamp[:, :, :].rearrange("p a b -> p (a b)"), b_("lamq", T), b_("lamk", T),
                                        ALU.mult).then_inc(lam_s, 1)
                dve.wait_ge(lam_s, 1)
                nc.vector.tensor_reduce(lamd[:, :], lamp[:, :, :], AX.X, ALU.add).then_inc(lam_s, 1)
                nc.vector.memset(coef[:, 0:1], 1.0 - LAMBDA_INIT).then_inc(coef_done, 1)
                nc.vector.tensor_tensor(xbo[:, :], a_("x")[0:T, :], b_("bo", T), ALU.add).then_inc(xbo_done, 1)

            def lambda_coefficients():
                dve.wait_ge(lam_e, 1)
                nc.vector.tensor_tensor(lamx[:, :], lame[:, 1:2], lame[:, 0:1], ALU.subtract).then_inc(lam_s, 1)
                dve.wait_ge(lam_s, 3)
                nc.vector.tensor_scalar(coef[:, 1:2], lamx[:, :], -LAMBDA_INIT, 1.0 - LAMBDA_INIT,
                                        ALU.add, ALU.mult).then_inc(coef_done, 1)
                dve.wait_ge(coef_done, 2)
                nc.vector.tensor_scalar(vsc[:, :], coef[:, 1:2], 1.0 - LAMBDA_INIT, None,
                                        ALU.add).then_inc(lam_s, 1)
                dve.wait_ge(lam_s, 4)
                nc.vector.tensor_scalar(vbt[:, :], b_("vb", T), vsc[:, 0:1], None, ALU.mult).then_inc(vbt_done, 1)

            def slot(g, par, last, last_but_one):
                for c in range(CHUNKS):
                    if c < CHUNKS - 1 and not last:
                        for h in range(2):
                            chunk_max(g + 1, c + 1, h, 1 - par)
                    if c == CHUNKS - 1 and not last:
                        group_max(g + 1, 1 - par)
                        if not last_but_one:
                            for h in range(2):
                                chunk_max(g + 2, 0, h, par)
                save_sums(g)

            with dve.Fori(0, (GROUPS - 2) // 2) as it:
                for par in range(2):
                    slot(2 * it + par, par, False, False)
            lambda_dots()
            slot(GROUPS - 2, 0, False, True)
            lambda_coefficients()
            slot(GROUPS - 1, 1, True, False)
            tail_dve(dve)

        @block.tensor
        def _(pe):
            def project_keys(u):
                if u % 2 == 0:
                    pe.wait_ge(ctx_in_s[u // 2], 16)
                if u >= RING:
                    pe.wait_ge(klo_done, u - RING + 1)
                pe.matmul(ring[:, u % RING, 0:HALF], wk16[:, :], ctxT[:, HALF * u:HALF * u + HALF],
                          start=True, stop=True).then_inc(lg_full, 1)

            def project_values(v):
                c, j = divmod(v, 2)
                i = 2 * CHUNKS + v
                if v < RING:
                    pe.wait_ge(klo_done, i - RING + 1)
                else:
                    pe.wait_ge(act_done, i - RING + 1)
                t0, nt = ((0, 4), (4, 3))[j]
                for t in range(nt):
                    k = P * (TPC * c + t0 + t)
                    last = pe.matmul(ring[:, i % RING, P * t:P * t + P], ctxT[:, k:k + P], b_("wv"),
                                     start=True, stop=True)
                last.then_inc(lg_full, 1)

            def pass1(g, c, h, par, arrived):
                if h == 0:
                    pe.wait_ge(kst_in[par][c], arrived)
                if not (isinstance(g, int) and chunk_no(g, c, h) < 2):
                    pe.wait_ge(p1_empty, chunk_no(g, c, h) - 1)
                q = qs[:, bass.ds(g, 1), T * 2 * h:T * 2 * h + 2 * T].rearrange("p g n -> p (g n)")
                for i in range(2):
                    k = CK * c + HALF * i
                    last = pe.matmul(p1[:, h, i, 0:HALF], q, kst[:, par, k:k + HALF], start=True, stop=True)
                last.then_inc(p1_full, 1)

            def pass2(g, c, e, par):
                k = EPC * c + e
                if k >= RING:
                    pe.wait_ge(act_done, entry_no(g, c, e) - RING + 1)
                elif k == 0:
                    pe.wait_ge(act_done, entry_no(g, 0, 0))
                q = qs[:, bass.ds(g, 1), :].rearrange("p g n -> p (g n)")
                for i in range(ENTRY_TILES[e]):
                    t = TPC * c + ENTRY0[e] + i
                    last = pe.matmul(ring[:, k % RING, COLS * i:COLS * i + COLS],
                                     kst[:, par, P * t:P * t + P], q, start=True, stop=True)
                last.then_inc(lg_full, 1)

            def values(g, c, par, it):
                if c == 0:
                    pe.wait_ge(v_in[par], 16 * it + 16)
                    pe.wait_ge(acc_free, g + 1)
                for e in range(EPC):
                    k = EPC * c + e
                    pe.wait_ge(act_done, entry_no(g, c, e + 1))
                    for i in range(ENTRY_TILES[e]):
                        t = TPC * c + ENTRY0[e] + i
                        j = BLK * (t % 4)
                        last = pe.matmul(acc[j:j + 2 * VW, 0:COLS], vcur[:, par, t, :],
                                         probs[:, (EPC * CHUNKS * par + k) % PROBS, COLS * i:COLS * i + COLS],
                                         start=(t < 4), stop=(t >= KT - 4))
                    last.then_inc(probs_free, 1)

            def max_row(g, par):
                pe.wait_ge(m_ready, g + 1)
                pe.wait_ge(act_done, entry_no(g - 1, CHUNKS, 0) - RING + 1)
                for h in range(2):
                    last = pe.matmul(ring[0:1, MROW % RING, P * h:P * h + P], negmax16[:, par, h:h + 1],
                                     ident16[:, :], start=True, stop=True)
                last.then_inc(lg_full, 1)

            pe.wait_ge(wk_done, 2)
            for u in range(3):
                project_keys(u)
            pe.wait_ge(xn_done, 1)
            pe.transpose(p1[:, 0, 0, 0:T], xn[:, :], ident[0:T, 0:T]).then_inc(xnT_ps, 1)
            project_keys(3)
            pe.wait_ge(wq_in, 16)
            pe.wait_ge(xnT_done, 1)
            for g in range(GROUPS):
                last = pe.matmul(p1[0:STK, 0, 1, T * g:T * g + T], a_("wq")[:, STK * g:STK * g + STK], xnT[:, :],
                                 start=True, stop=True)
            last.then_inc(q_ps, 1)
            for u in range(4, LEAD):
                project_keys(u)
            pe.wait_ge(q0_done, 1)
            pe.wait_ge(qs_zero, 1)
            pe.wait_ge(kst_set, 2)
            v = 0
            for c in range(CHUNKS):
                for h in range(2):
                    pass1(0, c, h, 0, 16)
                    u = 2 * c + h + LEAD
                    if u < 2 * CHUNKS:
                        project_keys(u)
                if u >= 2 * CHUNKS:
                    if v == 0:
                        pe.wait_ge(b_in_s, 16)
                    for _ in range(3):
                        project_values(v)
                        v += 1
            pe.wait_ge(q_done, 1)
            for h in range(2):
                pass1(1, 0, h, 1, 16)
            while v < 2 * CHUNKS:
                project_values(v)
                v += 1
            pe.wait_ge(id16_done, 1)
            max_row(0, 0)
            pe.wait_ge(d_in_s, 16)
            pe.wait_ge(acc_free, 1)
            pe.matmul(acc[0:H, COLS:COLS + 2 * T - 1], d_("table", 32), d_("onehot", 32),
                      start=True, stop=True).then_inc(rel_ps, 1)
            pe.wait_ge(rel_sb, 1)

            def slot(g, par, it, last, last_but_one):
                for c in range(CHUNKS):
                    for h in range(2):
                        if c < CHUNKS - 1 and not last:
                            pass1(g + 1, c + 1, h, 1 - par, stacked(it, par, 1))
                        pass2(g, c, 2 * h, par)
                        pass2(g, c, 2 * h + 1, par)
                    if c > 0:
                        values(g, c - 1, par, it)
                if not last:
                    max_row(g + 1, 1 - par)
                    if not last_but_one:
                        for h in range(2):
                            pass1(g + 2, 0, h, par, stacked(it, par, 2))
                values(g, CHUNKS - 1, par, it)

            with pe.Fori(0, (GROUPS - 2) // 2) as it:
                for par in range(2):
                    slot(2 * it + par, par, it, False, False)
            slot(GROUPS - 2, 0, (GROUPS - 2) // 2, False, True)
            expert_bias(pe)
            slot(GROUPS - 1, 1, (GROUPS - 2) // 2, True, False)
            tail_pe(pe)


def _buckets():
    half, exact, far = 16, 8, 128
    out = []
    for d in range(1 - T, T):
        n = abs(d)
        large = exact + int(np.float32(np.log(np.float32(max(n, 1)) / np.float32(exact)))
                            / np.float32(np.log(far / exact)) * np.float32(half - exact))
        out.append((half if d > 0 else 0) + (n if n < exact else min(large, half - 1)))
    return out


def _pack(cols, total, rows, parts):
    a = np.zeros((rows, total), np.float32)
    for k, v in parts.items():
        a[0:v.shape[0], cols[k][0]:cols[k][1]] = v
    return a


def kernel(**inputs):
    import concourse.bacc as _bacc
    from concourse.bass_utils import run_bass_kernel_spmd as _run

    i = {k: np.asarray(v) for k, v in inputs.items()}
    L = "L0_"
    inw, inb = i[L + "xattn_in_proj_weight"].T, i[L + "xattn_in_proj_bias"]
    r = np.arange(P)
    row = np.arange(STK) % (2 * GD) // 2
    maskq = (row[:, None] // SUB == np.arange(4)[None, :])
    dims = GD * np.arange(GROUPS)[:, None] + row[None, :]
    sel = np.zeros((P, 2 * VW), np.float32)
    for j in range(4):
        sel[BLK * j + np.arange(2 * VW), np.arange(2 * VW)] = 1
    maskk = (r[:, None] // HD % (H // 2) == np.arange(H // 2)[None, :])
    tri = np.broadcast_to((np.arange(E)[None, :] < np.arange(E)[:, None]).reshape(1, E * E), (P, E * E))
    onehot = (np.arange(32)[:, None] == np.array(_buckets())[None, :])
    a = _pack(A_AT, A_N, P, dict(x=i["x"][0], ident=np.eye(P), bk=inb[D:2 * D, None], bq=inb[0:D][dims.T],
                                 maskq=maskq, wk=inw[:, D:2 * D], wq=inw[:, 0:D][:, dims.ravel()]))
    b = _pack(B_AT, B_N, P, dict(
        wv=inw[:, 2 * D:3 * D], sel=sel, vb=np.broadcast_to(inb[2 * D:], (T, D)),
        bo=np.broadcast_to(i[L + "xattn_out_proj_bias"], (T, D)),
        lamq=np.broadcast_to(np.concatenate([i[L + "xattn_lambda_q1"], i[L + "xattn_lambda_q2"]]), (T, 2 * SUB)),
        lamk=np.broadcast_to(np.concatenate([i[L + "xattn_lambda_k1"], i[L + "xattn_lambda_k2"]]), (T, 2 * SUB)),
        wo=i[L + "xattn_out_proj_weight"].T, awq=i[L + "attn_w_q"].T, awk=i[L + "attn_w_k"].T,
        awv=i[L + "attn_w_v"].T, awo=i[L + "attn_w_o"].T, maskk=maskk, tri=tri, pair=np.tile(np.eye(T), (2, 1)), flip=np.kron(np.eye(2), np.eye(T)[::-1])))
    eb1 = i[L + "ffn_eb1"].reshape(4, 2 * FC, P)
    d = _pack(D_AT, D_N, 32, dict(
        table=i[L + "attn_rel_bias_table"], onehot=onehot, blk=np.repeat(np.eye(FC), P, axis=1),
        blk8=np.repeat(np.eye(8), T, axis=1), rb1=i[L + "ffn_rb1"].reshape(FC, P),
        eb1=eb1.transpose(1, 0, 2).reshape(2 * FC, 4 * P), parsel=np.repeat(np.eye(2), T, axis=1),
        eb2=i[L + "ffn_eb2"].reshape(4, 2, D).transpose(1, 0, 2).reshape(2, 4 * D),
        ones=np.ones((1, P)), rb2=i[L + "ffn_rb2"].reshape(1, E)))
    arrays = dict(
        a_in=a, ctx_in=i["ctx_1024"][0].T, b_in=b,
        ew1_in=i[L + "ffn_ew1"].transpose(1, 0, 2).reshape(P, E * FH),
        ew2_in=i[L + "ffn_ew2"].reshape(E, FC, P, D).transpose(2, 0, 1, 3).reshape(P, E * FC * D),
        rw1_in=i[L + "ffn_rw1"], rw2_in=i[L + "ffn_rw2"].reshape(FC, P, E).transpose(1, 0, 2).reshape(P, FC * E),
        d_in=d)
    arrays = {k: np.ascontiguousarray(v) for k, v in arrays.items()}
    nc = _bacc.Bacc("TRN2", target_bir_lowering=False, num_devices=1)
    args = [nc.dram_tensor(k, v.shape, F32, kind="ExternalInput").ap() for k, v in arrays.items()]
    scratch = nc.dram_tensor("relative_bias", (H, 2 * T - 1), F32, kind="Internal").ap()
    kparts = nc.dram_tensor("key_parts", (D, 2, S), F16, kind="Internal").ap()
    out = nc.dram_tensor("out_dram", (T, D), F32, kind="ExternalOutput").ap()
    perceiver_layer(nc, *args, scratch, kparts, out)
    got = _run(nc, [arrays], core_ids=[0])
    return got.results[0]["out_dram"].reshape(1, T, D)
```

```python
from contextlib import ExitStack

import numpy as np

import concourse.bass as bass
from concourse import mybir

F32 = mybir.dt.float32
F16 = mybir.dt.float16
U32 = mybir.dt.uint32
ALU = mybir.AluOpType
ACT = mybir.ActivationFunctionType
AX = mybir.AxisListType

P = 128
T = 64
S = 6272
D = 128
H = 16
HD = D // H
SUB = HD // 2
GROUPS = H // 2
GD = 2 * HD
BLK = 32
STK = 4 * GD
CHUNKS = 7
CK = S // CHUNKS
HALF = CK // 2
KT = S // P
TPC = KT // CHUNKS
ENTRY_TILES = [2, 2, 2, 1]
ENTRY0 = [0, 2, 4, 6]
EPC = len(ENTRY_TILES)
COLS = 2 * 2 * T
PER_SLOT = EPC * CHUNKS + 1
MROW = EPC * CHUNKS
RING = 3
PROBS = 8
VW = HD + 1
SCALE_IN = 16.0
MSCALE = SCALE_IN * SCALE_IN
MPAIR = float(np.array([MSCALE, MSCALE], np.float16).view(np.float32)[0])
EPS = 1e-5
LAMBDA_INIT = 0.8 - 0.6
E = 8
FH = 512
FC = FH // P
WSCALE = 16.0
N1 = FH + E * FH
N2 = E * FC * D
STAGE = 1024
LEAD = 10

A_COLS = dict(x=D, ident=P, bk=1, bq=GROUPS, maskq=4, wk=D, wq=GROUPS * STK)
A_FIRST = A_COLS["x"] + A_COLS["ident"] + 1 + GROUPS + 4
B_COLS = dict(wv=D, sel=2 * VW, vb=D, bo=D, lamq=2 * SUB, lamk=2 * SUB, wo=D, awq=D, awk=D, awv=D, awo=D,
              maskk=H // 2, tri=E * E, flip=P, rw2=FC * E)
D_COLS = dict(table=H, onehot=2 * T - 1, blk=E * T, blk2=E * T, rb1=P, eb1=4 * P, eb2=D, ones=P, rb2=E)


def offsets(cols):
    out, at = {}, 0
    for k, n in cols.items():
        out[k] = (at, at + n)
        at += n
    return out, at


A_AT, A_N = offsets(A_COLS)
B_AT, B_N = offsets(B_COLS)
D_AT, D_N = offsets(D_COLS)


def perceiver_layer(nc, a_in, ctx_in, b_in, w1_in, w2_in, d_in, bias_scratch, kparts_dram, out):
    with ExitStack() as ctx:
        def sb(name, shape, dt=F32):
            return ctx.enter_context(nc.sbuf_tensor(name, shape, dt))

        def sem(name):
            return ctx.enter_context(nc.semaphore(name))

        wa = sb("wa", [P, A_N])
        wb = sb("wb", [P, B_N])
        wd = sb("wd", [32, D_N])
        ctxT = sb("ctxT", [P, S])
        kparts = sb("kparts", [P, 2, S], F16)
        kst = sb("kst", [P, 2, S], F16)
        qs = sb("qs", [P, GROUPS, COLS], F16)
        vall = sb("vall", [P, GROUPS, KT, 2 * VW])
        vcur = sb("vcur", [P, 2, KT, 2 * VW])
        probs = sb("probs", [P, PROBS, 2 * COLS])
        accs = sb("accs", [P, GROUPS, COLS])
        w1p = kparts[:, :, :].rearrange("p a n -> p (a n)")[:, 0:2 * N1].rearrange("p (a n) -> p a n", a=2)
        w2p = ctxT[:, 0:N2].bitcast(F16).rearrange("p (a n) -> p a n", a=2)
        stage = ctxT[:, N2:N2 + 2 * STAGE].rearrange("p (a n) -> p a n", a=2)
        ident16 = sb("ident16", [P, P], F16)
        wk16 = sb("wk16", [P, D])
        bk16 = sb("bk16", [P, 1])
        stats = sb("stats", [T, 6])
        mv = sb("mv", [T, 2])
        rstd = sb("rstd", [T, 1])
        veps = sb("veps", [T, 1])
        power = sb("power", [T, 1])
        xn = sb("xn", [T, D])
        xnT = sb("xnT", [P, T])
        bq16 = sb("bq16", [STK, GROUPS])
        qf = sb("qf", [STK, GROUPS, T])
        qparts = sb("qparts", [STK, GROUPS, T], F16)
        mx = sb("mx", [P, 2, 2, CHUNKS])
        negmax = sb("negmax", [P, 2])
        negmax16 = sb("negmax16", [P, 2, 2], F16)
        lamp = sb("lamp", [T, 2, SUB])
        lamd = sb("lamd", [T, 2])
        lame = sb("lame", [T, 2])
        lamx = sb("lamx", [T, 1])
        spare = sb("spare", [1, 1])
        spare2 = sb("spare2", [1, 1])
        coef = sb("coef", [T, 2])
        vsc = sb("vsc", [T, 1])
        vbt = sb("vbt", [T, D])
        xbo = sb("xbo", [T, D])
        rec = sb("rec", [T, H, 2])
        o4 = sb("o4", [T, H, 2, HD])
        osum = sb("osum", [T, D])
        attn = sb("attn", [T, D])
        attnT = sb("attnT", [P, T])
        x1 = sb("x1", [T, D])
        x1T = sb("x1T", [P, 2, T])
        qTs = sb("qTs", [P, T])
        kbd = sb("kbd", [P, H // 2, T])
        vbd = sb("vbd", [P, H // 2, 2, VW])
        relT = sb("relT", [H, 2 * T - 1])
        relb = sb("relb", [P, H // 2, T])
        smx = sb("smx", [P, H // 2])
        ssub = sb("ssub", [P, H // 2, T])
        sexp = sb("sexp", [P, H // 2, T])
        pT = sb("pT", [P, 4, 2, T])
        rec2 = sb("rec2", [T, H])
        attn2 = sb("attn2", [T, D])
        attn2T = sb("attn2T", [P, T])
        x2 = sb("x2", [T, D])
        x2T = sb("x2T", [P, 2, T], F16)
        hr = sb("hr", [P, FC, T])
        lg = sb("lg", [T, E])
        gt = sb("gt", [T, E, E])
        eq = sb("eq", [T, E, E])
        eqt = sb("eqt", [T, E, E])
        ahead = sb("ahead", [T, E, E])
        rank = sb("rank", [T, E])
        lmx = sb("lmx", [T, 1])
        lsub = sb("lsub", [T, E])
        lexp = sb("lexp", [T, E])
        sel2 = sb("sel2", [T, E])
        den = sb("den", [T, 1])
        rden = sb("rden", [T, 1])
        gdiag = sb("gdiag", [T, E, T])
        gall = sb("gall", [P, E, T])
        unscale = sb("unscale", [T, P])
        hs = sb("hs", [P, 4, 2, 8 * T], F16)
        gated = sb("gated", [P, E, T])
        ysum = sb("ysum", [P, T])
        y = sb("y", [T, D])

        def a_(k):
            return wa[:, A_AT[k][0]:A_AT[k][1]]

        def b_(k, n=P):
            return wb[0:n, B_AT[k][0]:B_AT[k][1]]

        def d_(k, n):
            return wd[0:n, D_AT[k][0]:D_AT[k][1]]

        ident = a_("ident")

        p1 = ctx.enter_context(nc.psum_tensor("p1", [P, 2, 2, 512], F32))
        ring = ctx.enter_context(nc.psum_tensor("ring", [P, RING, 512], F32))
        acc = ctx.enter_context(nc.psum_tensor("acc", [P, 512], F32))

        a_in_s = sem("a_loaded")
        b_in_s = sem("b_loaded")
        d_in_s = sem("d_loaded")
        w_in = [sem(f"weights_staged{n}") for n in range(2)]
        w_scaled = sem("weights_scaled")
        w_high = sem("weights_high_part")
        w_split = sem("weights_split")
        unscale_set = sem("unscale_set")
        table_in = sem("spare_set")
        ctx_in_s = [sem(f"ctx_loaded{c}") for c in range(CHUNKS)]
        kst_in = [[sem(f"keys_stacked{p}_{c}") for c in range(CHUNKS)] for p in range(2)]
        k_out = [sem(f"keys_spread{c}") for c in range(CHUNKS)]
        wk_in = sem("wk_loaded")
        wq_in = sem("wq_loaded")
        v_in = [sem(f"values_in{p}") for p in range(2)]
        qs_zero = sem("qs_zeroed")
        kst_set = sem("kst_row_set")
        ones_set = sem("ones_set")
        ln_s = sem("ln_steps")
        veps_done = sem("variance_with_eps")
        power_set = sem("power_set")
        xn_done = sem("xn_done")
        xnT_ps = sem("xnT_in_psum")
        xnT_done = sem("xnT_done")
        q_ps = sem("q_in_psum")
        id16_done = sem("ident16_done")
        wk_done = sem("wk_scaled")
        q_read = sem("q_out_of_psum")
        qsplit = sem("q_split_steps")
        q0_done = sem("queries0_done")
        q_done = sem("queries_done")
        klo_done = sem("klo_done")
        p1_full = sem("pass1_full")
        p1_empty = sem("pass1_reduced")
        nm_raw = sem("negmax_done")
        m_ready = sem("negmax16_ready")
        lg_full = sem("logits_full")
        act_done = sem("ring_entry_read")
        probs_free = sem("probs_free")
        acc_free = sem("sums_bank_free")
        lam_s = sem("lambda_steps")
        lam_e = sem("lambda_exp")
        coef_done = sem("coef_done")
        vbt_done = sem("vbt_done")
        xbo_done = sem("xbo_done")
        vbd_zero = sem("vbd_zeroed")
        vbd_ones = sem("vbd_ones_set")
        po_ps = sem("attention_sums_in_psum")
        norm_s = sem("normalise_steps")
        attn_done = sem("attn_done")
        attnT_ps = sem("attnT_in_psum")
        attnT_done = sem("attnT_done")
        proj1_ps = sem("cross_attention_in_psum")
        x1_done = sem("x1_done")
        qk_ps = sem("self_qk_in_psum")
        v_ps = sem("self_v_in_psum")
        qk_done = sem("self_qk_done")
        vbd_done = sem("self_v_done")
        sc_ps = sem("self_scores_in_psum")
        smx_done = sem("self_max_done")
        ssub_done = sem("self_shifted")
        sexp_done = sem("self_exp_done")
        pT_ps = sem("self_probsT_in_psum")
        pT_done = sem("self_probsT_done")
        pv_ps = sem("self_values_in_psum")
        rec2_done = sem("self_reciprocal_done")
        attn2_done = sem("self_attn_done")
        attn2T_ps = sem("self_attnT_in_psum")
        attn2T_done = sem("self_attnT_done")
        proj2_ps = sem("self_attention_in_psum")
        x2_done = sem("x2_done")
        hr_ps = sem("router_hidden_in_psum")
        hr_done = sem("router_hidden_done")
        lg_ps = sem("router_logits_in_psum")
        gate_s = sem("gate_steps")
        lexp_done = sem("router_exp_done")
        gate_done = sem("gates_done")
        he_ps = sem("expert_hidden_in_psum")
        hs_done = sem("expert_hidden_done")
        eo_ps = sem("expert_out_in_psum")
        hl_done = sem("expert_hidden_low_done")
        gdiag_done = sem("gates_spread")
        gall_ps = sem("gates_in_psum")
        gall_done = sem("gates_on_all_partitions")
        gated_done = sem("gated_done")
        ysum_done = sem("mixture_summed")
        y_ps = sem("mixture_in_psum")
        y_done = sem("y_done")
        out_done = sem("out_written")
        rel_ps = sem("rel_in_psum")
        rel_sb = sem("rel_in_sbuf")
        rel_out = sem("rel_in_dram")
        rel_in = sem("rel_spread")

        block = ctx.enter_context(nc.Block())

        def chunk_no(g, c, h):
            return 2 * CHUNKS * g + 2 * c + h

        def entry_no(g, c, e):
            return PER_SLOT * (g + 1) + EPC * c + e

        def products_done(g):
            return PROBS + EPC * CHUNKS * (g + 1)

        def stacked(it, par, ahead_by):
            return (it + (par + ahead_by) // 2 + 1) * 16

        def bank(i):
            return p1[:, i // 2, i % 2, :] if i < 4 else ring[:, i - 4, :] if i < 7 else acc[:, :]

        po = bank(0)[0:T, 0:2 * H * VW].rearrange("p (h s v) -> p h s v", h=H, s=2)
        pv = bank(4)[0:T, 0:H * VW].rearrange("p (h v) -> p h v", h=H)
        sc = bank(6).rearrange("p (h k) -> p h k", h=H // 2)
        SPLITS = [(p, n, min(n + STAGE, total)) for p, total in enumerate((N1, N2)) for n in range(0, total, STAGE)]
        ALL_READ = PER_SLOT * (GROUPS + 1) - 1

        def last_logits(k):
            return bank((4, 5, 6, 2, 3)[k % 5])

        def sums(pe, g):
            pe.wait_ge(acc_free, g + 2)
            for h in range(2):
                for s in range(2):
                    i = (2 * g + h) * 2 + s
                    k = T * (2 * h + s)
                    last = pe.matmul(bank(0)[0:T, VW * i:VW * i + VW], accs[:, g, k:k + T],
                                     b_("sel")[:, VW * h:VW * h + VW], start=True, stop=True)
            return last

        def expert_bias(pe, b):
            pe.matmul(bank(b), d_("eb1", 8)[:, P * b:P * b + P], d_("blk", 8), start=True, stop=False,
                      skip_group_check=True)

        def split_products(pe, out, w, x, stop_last=True):
            for wn in range(2):
                for xn_ in range(2):
                    last = pe.matmul(out, w(wn), x(xn_), start=False, stop=True, skip_group_check=True)
            return last

        def tail_pe(pe):
            sums(pe, GROUPS - 1).then_inc(po_ps, 1)
            pe.wait_ge(act_done, ALL_READ)
            pe.wait_ge(rel_in, 32)
            pe.matmul(bank(6), b_("flip"), relb[:, :, :].rearrange("p h k -> p (h k)"), start=True, stop=False,
                      skip_group_check=True)
            pe.wait_ge(attn_done, 1)
            pe.transpose(bank(5)[:, 0:T], attn[:, :], ident[0:T, 0:T]).then_inc(attnT_ps, 1)
            pe.wait_ge(attnT_done, 1)
            pe.matmul(bank(7)[0:T, 0:D], attnT[:, :], b_("wo"), start=True, stop=True).then_inc(proj1_ps, 1)
            for b in (1, 2):
                expert_bias(pe, b)
            pe.wait_ge(xn_done, 2)
            pe.transpose(bank(5)[:, 0:T], xn[:, :], ident[0:T, 0:T]).then_inc(xnT_ps, 1)
            pe.wait_ge(xnT_done, 2)
            pe.matmul(bank(4)[:, 0:T], b_("awq"), x1T[:, 0, :], start=True, stop=True)
            pe.matmul(bank(4)[:, T:2 * T], b_("awk"), x1T[:, 0, :], start=True, stop=True).then_inc(qk_ps, 1)
            pe.wait_ge(x1_done, 1)
            pe.matmul(bank(7)[:, 0:D], x1T[:, :, :].rearrange("p a t -> p (a t)"), b_("awv"),
                      start=True, stop=True).then_inc(v_ps, 1)
            pe.wait_ge(qk_done, 2)
            for half in range(2):
                r = T * half
                last = pe.matmul(bank(6)[r:r + T, :], qTs[r:r + T, :],
                                 kbd[r:r + T, :, :].rearrange("p h k -> p (h k)"), start=False, stop=True,
                                 skip_group_check=True)
            last.then_inc(sc_ps, 1)
            for b in (0, 3):
                expert_bias(pe, b)
            pe.wait_ge(sexp_done, 1)
            pe.wait_ge(vbd_done, 2)
            for n in range(4):
                last = pe.transpose(bank(5 + 2 * (n // 2))[:, P * (n % 2):P * (n % 2) + P],
                                    sexp[:, 2 * n:2 * n + 2, :].rearrange("p h k -> p (h k)"), ident)
            last.then_inc(pT_ps, 1)
            pe.wait_ge(pT_done, 2)
            for n in range(H // 2):
                last = pe.matmul(bank(4)[0:T, 2 * VW * n:2 * VW * n + 2 * VW], pT[:, n % 4, n // 4, :],
                                 vbd[:, n, :, :].rearrange("p a v -> p (a v)"), start=True, stop=True)
            last.then_inc(pv_ps, 1)
            pe.wait_ge(attn2_done, 1)
            pe.transpose(bank(5)[:, 0:T], attn2[:, :], ident[0:T, 0:T]).then_inc(attn2T_ps, 1)
            pe.wait_ge(attn2T_done, 1)
            pe.matmul(bank(4)[0:T, 0:D], attn2T[:, :], b_("awo"), start=True, stop=True).then_inc(proj2_ps, 1)
            pe.matmul(bank(6)[:, 0:FC * T], d_("rb1", FC), d_("blk", FC)[:, 0:FC * T], start=True, stop=False,
                      skip_group_check=True)
            pe.matmul(bank(7), d_("eb2", E), d_("blk2", E), start=True, stop=False, skip_group_check=True)
            pe.wait_ge(xn_done, 3)
            pe.transpose(bank(5)[:, 0:T], xn[:, :], ident[0:T, 0:T]).then_inc(xnT_ps, 1)
            pe.wait_ge(w_split, len(SPLITS))
            pe.wait_ge(xnT_done, 4)
            for f in range(FC):
                last = split_products(pe, bank(6)[:, T * f:T * f + T],
                                      lambda n: w1p[:, n, P * f:P * f + P], lambda n: x2T[:, n, :])
            last.then_inc(hr_ps, 1)

            def expert_hidden(b):
                for n in range(8):
                    k = FH + (8 * b + n) * P
                    last = split_products(pe, bank(b)[:, T * n:T * n + T],
                                          lambda m: w1p[:, m, k:k + P], lambda m: x2T[:, m, :])
                last.then_inc(he_ps, 1)

            def expert_out(b):
                pe.wait_ge(hl_done, b + 1)
                for n in range(8):
                    e, f = 2 * b + n // FC, n % FC
                    k = (e * FC + f) * D
                    last = split_products(pe, bank(7)[:, T * e:T * e + T],
                                          lambda m: w2p[:, m, k:k + D], lambda m: hs[:, b, m, T * n:T * n + T])
                return last

            expert_hidden(0)
            pe.wait_ge(hr_done, 1)
            pe.matmul(bank(5)[0:T, 0:E], d_("ones", 1)[:, 0:T], d_("rb2", 1), start=True, stop=False)
            for f in range(FC):
                last = pe.matmul(bank(5)[0:T, 0:E], hr[:, f, :], b_("rw2")[:, E * f:E * f + E],
                                 start=False, stop=(f == FC - 1))
            last.then_inc(lg_ps, 1)
            for b in range(1, 4):
                expert_hidden(b)
            for b in range(2):
                expert_out(b)
            pe.wait_ge(gdiag_done, 1)
            pe.wait_ge(unscale_set, 1)
            pe.matmul(bank(4), unscale[:, :], gdiag[:, :, :].rearrange("p e t -> p (e t)"), start=True,
                      stop=True).then_inc(gall_ps, 1)
            expert_out(2)
            expert_out(3).then_inc(eo_ps, 1)
            pe.wait_ge(ysum_done, 1)
            pe.transpose(bank(5)[0:T, 0:D], ysum[:, :], ident).then_inc(y_ps, 1)

        def tail_act(act):
            act.wait_ge(vbd_ones, 2)
            act.wait_ge(v_ps, 1)
            for h2 in range(2):
                r = T * h2
                nc.scalar.copy(vbd[r:r + T, :, h2, 0:HD],
                               bank(7)[r:r + T, 0:D].rearrange("p (n h v) -> p n h v", h=2, v=HD)[:, :, h2, :]
                               ).then_inc(vbd_done, 1)
            act.wait_ge(ssub_done, 1)
            nc.scalar.activation(sexp[:, :, :], ssub[:, :, :], ACT.Exp).then_inc(sexp_done, 1)
            act.wait_ge(pT_ps, 1)
            nc.scalar.copy(pT[:, 2:4, :, :].rearrange("p a b t -> p (a b t)"), bank(7)[:, 0:2 * P]).then_inc(pT_done, 1)
            act.wait_ge(hr_ps, 1)
            nc.scalar.activation(hr[:, :, :].rearrange("p f t -> p (f t)"), bank(6)[:, 0:FC * T], ACT.Relu,
                                 scale=1.0 / WSCALE).then_inc(hr_done, 1)
            for b in range(4):
                act.wait_ge(he_ps, b + 1)
                nc.scalar.activation(hs[:, b, 0, :], bank(b), ACT.Relu).then_inc(hs_done, 1)
                if b == 1:
                    act.wait_ge(gate_s, 3)
                    nc.scalar.activation(lexp[:, :], lsub[:, :], ACT.Exp).then_inc(lexp_done, 1)
            act.wait_ge(gall_ps, 1)
            nc.scalar.copy(gall[:, :, :].rearrange("p e t -> p (e t)"), bank(4)).then_inc(gall_done, 1)

        def deviation(pool, n):
            pool.wait_ge(ln_s, 3 * n + 2)
            nc.gpsimd.tensor_scalar(veps[:, :], mv[:, 1:2], EPS, None, ALU.add).then_inc(veps_done, 1)
            pool.wait_ge(veps_done, n + 1)
            nc.gpsimd.tensor_tensor(rstd[:, :], veps[:, :], power[:, :], ALU.pow).then_inc(ln_s, 1)

        def layer_norm(dve, x, n):
            nc.vector.bn_stats(stats[:, :], x).then_inc(ln_s, 1)
            dve.wait_ge(ln_s, 3 * n + 1)
            nc.vector.bn_aggr(mv[:, :], stats[:, :]).then_inc(ln_s, 1)
            dve.wait_ge(ln_s, 3 * n + 3)
            nc.vector.tensor_scalar(xn[:, :], x, mv[:, 0:1], rstd[:, 0:1],
                                    ALU.subtract, ALU.mult).then_inc(xn_done, 1)

        def tail_dve(dve):
            dve.wait_ge(po_ps, 1)
            nc.vector.reciprocal(rec[:, :, :], po[:, :, :, HD]).then_inc(norm_s, 1)
            dve.wait_ge(norm_s, 1)
            nc.vector.tensor_tensor(rec[:, :, :], rec[:, :, :], coef[:, :].unsqueeze(1).to_broadcast([T, H, 2]),
                                    ALU.mult).then_inc(norm_s, 1)
            dve.wait_ge(norm_s, 2)
            nc.vector.tensor_tensor(o4[:, :, :, :], po[:, :, :, 0:HD],
                                    rec[:, :, :].unsqueeze(3).to_broadcast([T, H, 2, HD]), ALU.mult).then_inc(norm_s, 1)
            dve.wait_ge(norm_s, 3)
            nc.vector.tensor_tensor(osum[:, :].rearrange("p (h v) -> p h v", h=H), o4[:, :, 0, :], o4[:, :, 1, :],
                                    ALU.add).then_inc(norm_s, 1)
            dve.wait_ge(norm_s, 4)
            nc.vector.tensor_tensor(attn[:, :], osum[:, :], vbt[:, :], ALU.add).then_inc(attn_done, 1)
            dve.wait_ge(attnT_ps, 1)
            nc.vector.tensor_copy(attnT[:, :], bank(5)[:, 0:T]).then_inc(attnT_done, 1)
            dve.wait_ge(proj1_ps, 1)
            nc.vector.tensor_tensor(x1[:, :], bank(7)[0:T, 0:D], xbo[:, :], ALU.add).then_inc(x1_done, 1)
            dve.wait_ge(x1_done, 1)
            layer_norm(dve, x1[:, :], 1)
            dve.wait_ge(xnT_ps, 2)
            nc.vector.tensor_copy(x1T[:, :, :], bank(5)[:, 0:T].unsqueeze(1).to_broadcast([P, 2, T])).then_inc(xnT_done, 1)
            dve.wait_ge(qk_ps, 1)
            nc.vector.tensor_scalar(qTs[:, :], bank(4)[:, 0:T], HD ** -0.5, None, ALU.mult).then_inc(qk_done, 1)
            nc.vector.tensor_tensor(kbd[:, :, :], bank(4)[:, T:2 * T].unsqueeze(1).to_broadcast([P, H // 2, T]),
                                    b_("maskk").unsqueeze(2).to_broadcast([P, H // 2, T]), ALU.mult).then_inc(qk_done, 1)
            dve.wait_ge(sc_ps, 1)
            nc.vector.tensor_reduce(smx[:, :], sc, AX.X, ALU.max).then_inc(smx_done, 1)
            dve.wait_ge(smx_done, 1)
            nc.vector.tensor_tensor(ssub[:, :, :], sc, smx[:, :].unsqueeze(2).to_broadcast([P, H // 2, T]),
                                    ALU.subtract).then_inc(ssub_done, 1)
            dve.wait_ge(pT_ps, 1)
            nc.vector.tensor_copy(pT[:, 0:2, :, :].rearrange("p a b t -> p (a b t)"), bank(5)[:, 0:2 * P]).then_inc(pT_done, 1)
            dve.wait_ge(pv_ps, 1)
            nc.vector.reciprocal(rec2[:, :], pv[:, :, HD]).then_inc(rec2_done, 1)
            dve.wait_ge(rec2_done, 1)
            nc.vector.tensor_tensor(attn2[:, :].rearrange("p (h v) -> p h v", h=H), pv[:, :, 0:HD],
                                    rec2[:, :].unsqueeze(2).to_broadcast([T, H, HD]), ALU.mult).then_inc(attn2_done, 1)
            dve.wait_ge(attn2T_ps, 1)
            nc.vector.tensor_copy(attn2T[:, :], bank(5)[:, 0:T]).then_inc(attn2T_done, 1)
            dve.wait_ge(proj2_ps, 1)
            nc.vector.tensor_tensor(x2[:, :], bank(4)[0:T, 0:D], x1[:, :], ALU.add).then_inc(x2_done, 1)
            dve.wait_ge(x2_done, 1)
            layer_norm(dve, x2[:, :], 2)
            dve.wait_ge(xnT_ps, 3)
            nc.vector.tensor_copy(x2T[:, 0, :], bank(5)[:, 0:T]).then_inc(xnT_done, 1)
            dve.wait_ge(xnT_done, 3)
            nc.vector.tensor_tensor(x2T[:, 1, :], bank(5)[:, 0:T], x2T[:, 0, :], ALU.subtract).then_inc(xnT_done, 1)

            def low_hidden(b):
                dve.wait_ge(hs_done, b + 1)
                nc.vector.scalar_tensor_tensor(out=hs[:, b, 1, :], in0=bank(b), scalar=0.0, in1=hs[:, b, 0, :],
                                               op0=ALU.max, op1=ALU.subtract).then_inc(hl_done, 1)

            dve.wait_ge(lg_ps, 1)
            nc.vector.tensor_copy(lg[:, :], bank(5)[0:T, 0:E]).then_inc(gate_s, 1)
            dve.wait_ge(gate_s, 1)
            nc.vector.tensor_reduce(lmx[:, :], lg[:, :], AX.X, ALU.max).then_inc(gate_s, 1)
            dve.wait_ge(gate_s, 2)
            nc.vector.tensor_scalar(lsub[:, :], lg[:, :], lmx[:, 0:1], None, ALU.subtract).then_inc(gate_s, 1)
            other = lg[:, :].unsqueeze(1).to_broadcast([T, E, E])
            own = lg[:, :].unsqueeze(2).to_broadcast([T, E, E])
            nc.vector.tensor_tensor(gt[:, :, :], other, own, ALU.is_gt).then_inc(gate_s, 1)
            nc.vector.tensor_tensor(eq[:, :, :], other, own, ALU.is_equal).then_inc(gate_s, 1)
            dve.wait_ge(gate_s, 5)
            nc.vector.tensor_tensor(eqt[:, :, :].rearrange("p a b -> p (a b)"), eq[:, :, :].rearrange("p a b -> p (a b)"),
                                    b_("tri", T), ALU.mult).then_inc(gate_s, 1)
            dve.wait_ge(gate_s, 6)
            nc.vector.tensor_tensor(ahead[:, :, :], gt[:, :, :], eqt[:, :, :], ALU.add).then_inc(gate_s, 1)
            dve.wait_ge(gate_s, 7)
            nc.vector.tensor_reduce(rank[:, :], ahead[:, :, :], AX.X, ALU.add).then_inc(gate_s, 1)
            low_hidden(0)
            dve.wait_ge(gate_s, 8)
            dve.wait_ge(lexp_done, 1)
            nc.vector.scalar_tensor_tensor(out=sel2[:, :], in0=rank[:, :], scalar=2.0, in1=lexp[:, :],
                                           op0=ALU.is_lt, op1=ALU.mult).then_inc(gate_s, 1)
            dve.wait_ge(gate_s, 9)
            nc.vector.tensor_reduce(den[:, :], sel2[:, :], AX.X, ALU.add).then_inc(gate_s, 1)
            dve.wait_ge(gate_s, 10)
            nc.vector.reciprocal(rden[:, :], den[:, :]).then_inc(gate_s, 1)
            dve.wait_ge(gate_s, 11)
            nc.vector.scalar_tensor_tensor(
                out=gdiag[:, :, :], in0=sel2[:, :].unsqueeze(2).to_broadcast([T, E, T]), scalar=rden[:, 0:1],
                in1=ident[0:T, 0:T].unsqueeze(1).to_broadcast([T, E, T]), op0=ALU.mult, op1=ALU.mult
            ).then_inc(gdiag_done, 1)
            for b in range(1, 4):
                low_hidden(b)
            dve.wait_ge(gall_done, 1)
            dve.wait_ge(eo_ps, 1)
            nc.vector.tensor_tensor(gated[:, :, :].rearrange("p e t -> p (e t)"), bank(7),
                                    gall[:, :, :].rearrange("p e t -> p (e t)"), ALU.mult).then_inc(gated_done, 1)
            dve.wait_ge(gated_done, 1)
            nc.vector.tensor_reduce(ysum[:, :], gated[:, :, :].rearrange("p e t -> p t e"), AX.X,
                                    ALU.add).then_inc(ysum_done, 1)
            dve.wait_ge(y_ps, 1)
            nc.vector.tensor_tensor(y[:, :], bank(5)[0:T, 0:D], x2[:, :], ALU.add).then_inc(y_done, 1)

        @block.sync
        def _(sp):
            def stack_keys(g, c, par):
                k = kparts_dram[GD * g:GD * g + GD, :, CK * c:CK * c + CK]
                src = bass.AP(k.tensor, k.offset, [[0, 2], [S, 2 * GD], [1, CK]])
                sp.dma_start(kst[0:STK, par, CK * c:CK * c + CK], src).then_inc(kst_in[par][c], 16)

            for s0, s1, s in ((0, A_FIRST, a_in_s), (A_FIRST, A_FIRST + D, wk_in), (A_FIRST + D, A_N, wq_in)):
                sp.dma_start(wa[:, s0:s1], a_in[:, s0:s1]).then_inc(s, 16)
            for c in range(CHUNKS):
                sp.wait_ge(k_out[c], 16)
                for g in range(2):
                    stack_keys(g, c, g)
            sp.wait_ge(act_done, 28)
            for g in range(2):
                sp.dma_start(vcur[:, g, :, :], vall[:, g, :, :]).then_inc(v_in[g], 16)
            sp.wait_ge(rel_sb, 1)
            sp.dma_start(bias_scratch, relT[:, :]).then_inc(rel_out, 16)
            sp.wait_ge(rel_out, 16)
            n = 2 * T - 1
            for half in range(2):
                src = bass.AP(bias_scratch.tensor, bias_scratch.offset + half * (H // 2) * n,
                              [[1, T], [n, H // 2], [1, T]])
                sp.dma_start(relb[T * half:T * half + T, :, :], src).then_inc(rel_in, 16)
            for g in range(GROUPS - 2):
                for c in range(CHUNKS):
                    sp.wait_ge(lg_full, entry_no(g, c, EPC))
                    stack_keys(g + 2, c, g % 2)
                sp.wait_ge(probs_free, products_done(g))
                sp.dma_start(vcur[:, g % 2, :, :], vall[:, g + 2, :, :]).then_inc(v_in[g % 2], 16)
            sp.wait_ge(y_done, 1)
            sp.dma_start(out, y[:, :]).then_inc(out_done, 16)
            sp.wait_ge(out_done, 16)

        @block.gpsimd
        def _(pool):
            nc.gpsimd.memset(power[:, :], -0.5).then_inc(power_set, 1)
            nc.gpsimd.memset(qs[STK:P, :, :].rearrange("p g n -> p (g n)").bitcast(U32), 0).then_inc(qs_zero, 1)
            pool.wait_ge(power_set, 1)
            deviation(pool, 0)
            nc.gpsimd.memset(kst[STK:P, 1, :].bitcast(F32), MPAIR).then_inc(kst_set, 1)
            pool.wait_ge(qsplit, 3)
            nc.gpsimd.tensor_tensor(
                qs[0:STK, 1:GROUPS, :].rearrange("p g (a t) -> p g a t", a=4),
                qparts[:, 1:GROUPS, :].unsqueeze(2).to_broadcast([STK, GROUPS - 1, 4, T]),
                a_("maskq")[0:STK, :].unsqueeze(1).unsqueeze(3).to_broadcast([STK, GROUPS - 1, 4, T]),
                ALU.mult).then_inc(q_done, 1)
            pool.wait_ge(kst_set, 2)
            nc.gpsimd.memset(vall[:, :, :, :].rearrange("p g t v -> p (g t v)"), 1.0).then_inc(ones_set, 1)
            nc.gpsimd.memset(vbd[:, :, :, :].rearrange("p a b v -> p (a b v)"), 0.0).then_inc(vbd_zero, 1)
            pool.wait_ge(vbd_zero, 1)
            for h2 in range(2):
                nc.gpsimd.memset(vbd[T * h2:T * h2 + T, :, h2, HD:VW], 1.0).then_inc(vbd_ones, 1)
            nc.gpsimd.memset(spare2[:, :], 0.0).then_inc(probs_free, PROBS)
            nc.gpsimd.memset(unscale[:, :], 1.0 / WSCALE ** 2).then_inc(unscale_set, 1)
            for c in range(CHUNKS):
                pool.wait_ge(k_out[c], 16)
            pool.wait_ge(vbd_ones, 2)
            pool.wait_ge(unscale_set, 1)
            pool.wait_ge(act_done, 4 * CHUNKS)

            def load(n):
                p, k0, k1 = SPLITS[n]
                pool.dma_start(stage[:, n % 2, 0:k1 - k0], (w1_in, w2_in)[p][:, k0:k1]).then_inc(w_in[n % 2], 16)

            load(0)
            load(1)
            for n, (p, k0, k1) in enumerate(SPLITS):
                part = (w1p, w2p)[p]
                w = stage[:, n % 2, 0:k1 - k0]
                pool.wait_ge(w_in[n % 2], 16 * (n // 2 + 1))
                nc.gpsimd.tensor_scalar(w, w, WSCALE, None, ALU.mult).then_inc(w_scaled, 1)
                pool.wait_ge(w_scaled, n + 1)
                nc.gpsimd.tensor_copy(part[:, 0, k0:k1], w).then_inc(w_high, 1)
                pool.wait_ge(w_high, n + 1)
                nc.gpsimd.tensor_tensor(part[:, 1, k0:k1], w, part[:, 0, k0:k1], ALU.subtract).then_inc(w_split, 1)
                if n + 2 < len(SPLITS):
                    pool.wait_ge(w_split, n + 1)
                    load(n + 2)
            for n in (1, 2):
                deviation(pool, n)

        @block.scalar
        def _(act):
            for c in range(CHUNKS):
                act.dma_start(ctxT[:, CK * c:CK * c + CK], ctx_in[:, CK * c:CK * c + CK]).then_inc(ctx_in_s[c], 16)
            act.dma_start(wb[:, :], b_in).then_inc(b_in_s, 16)
            act.dma_start(wd[:, :], d_in).then_inc(d_in_s, 16)
            act.wait_ge(table_in, 1)
            nc.scalar.activation(spare[:, :], spare[:, :], ACT.Exp)
            act.wait_ge(wk_done, 2)

            def spread_keys(c):
                act.wait_ge(klo_done, 2 * c + 2)
                act.dma_start(kparts_dram[:, :, CK * c:CK * c + CK],
                              kparts[:, :, CK * c:CK * c + CK]).then_inc(k_out[c], 16)

            for u in range(2 * CHUNKS):
                act.wait_ge(lg_full, u + 1)
                nc.scalar.activation(kparts[:, 0, HALF * u:HALF * u + HALF], ring[:, u % RING, 0:HALF],
                                     ACT.Identity, bias=bk16[:, :]).then_inc(act_done, 1)
                if u >= 2 and u % 2 == 0:
                    spread_keys(u // 2 - 1)
            spread_keys(CHUNKS - 1)
            act.wait_ge(ones_set, 1)
            for c in range(CHUNKS):
                for j, (t0, nt) in enumerate(((0, 4), (4, 3))):
                    i = 2 * CHUNKS + 2 * c + j
                    act.wait_ge(lg_full, i + 1)
                    for t in range(nt):
                        last = nc.scalar.copy(
                            vall[:, :, TPC * c + t0 + t, :].rearrange("p g (h v) -> p g h v", v=VW)[:, :, :, 0:HD],
                            ring[:, i % RING, P * t:P * t + P].rearrange("p (g h v) -> p g h v", g=GROUPS, v=HD))
                    last.then_inc(act_done, 1)

            def max_row(g):
                act.wait_ge(lg_full, entry_no(g - 1, CHUNKS, 1))
                nc.scalar.copy(qs[STK:STK + 1, bass.ds(g, 1), :].rearrange("p g n -> p (g n)"),
                               ring[0:1, MROW % RING, 0:COLS]).then_inc(act_done, 1)

            def slot(g, par, last):
                for c in range(CHUNKS):
                    for e in range(EPC):
                        k = EPC * c + e
                        n = COLS * ENTRY_TILES[e]
                        act.wait_ge(lg_full, entry_no(g, c, e + 1))
                        act.wait_ge(probs_free, EPC * CHUNKS * g + k + 1)
                        src = last_logits(k) if last else ring[:, k % RING, :]
                        nc.scalar.activation(probs[:, (EPC * CHUNKS * par + k) % PROBS, 0:n], src[:, 0:n], ACT.Exp,
                                             scale=SUB ** -0.5 / MSCALE).then_inc(act_done, 1)
                if not last:
                    max_row(g + 1)

            act.wait_ge(q_done, 1)
            max_row(0)
            with act.Fori(0, (GROUPS - 2) // 2) as it:
                for par in range(2):
                    slot(2 * it + par, par, False)
            slot(GROUPS - 2, 0, False)
            act.wait_ge(lam_s, 2)
            nc.scalar.activation(lame[:, :], lamd[:, :], ACT.Exp).then_inc(lam_e, 1)
            slot(GROUPS - 1, 1, True)
            tail_act(act)

        @block.vector
        def _(dve):
            nc.vector.memset(spare[:, :], 0.0).then_inc(table_in, 1)
            nc.vector.memset(kst[STK:P, 0, :].bitcast(F32), MPAIR).then_inc(kst_set, 1)
            nc.vector.memset(acc[:, 0:COLS], 0.0).then_inc(acc_free, 1)
            dve.wait_ge(a_in_s, 16)
            nc.vector.bn_stats(stats[:, :], a_("x")[0:T, :]).then_inc(ln_s, 1)
            nc.vector.tensor_scalar(bk16[:, :], a_("bk"), SCALE_IN, None, ALU.mult).then_inc(wk_done, 1)
            dve.wait_ge(ln_s, 1)
            nc.vector.bn_aggr(mv[:, :], stats[:, :]).then_inc(ln_s, 1)
            dve.wait_ge(wk_in, 16)
            nc.vector.tensor_scalar(wk16[:, :], a_("wk"), SCALE_IN, None, ALU.mult).then_inc(wk_done, 1)
            nc.vector.tensor_scalar(bq16[:, :], a_("bq")[0:STK, :], SCALE_IN, None, ALU.mult).then_inc(qsplit, 1)
            nc.vector.tensor_copy(ident16[:, :], ident).then_inc(id16_done, 1)
            dve.wait_ge(ln_s, 3)
            nc.vector.tensor_scalar(xn[:, :], a_("x")[0:T, :], mv[:, 0:1], rstd[:, 0:1],
                                    ALU.subtract, ALU.mult).then_inc(xn_done, 1)

            def queries():
                half = slice(STK // 2, STK)
                dve.wait_ge(q_ps, 1)
                dve.wait_ge(qsplit, 1)
                nc.vector.scalar_tensor_tensor(
                    out=qf[:, :, :], in0=p1[0:STK, 0, 1, :].rearrange("p (g t) -> p g t", g=GROUPS), scalar=SCALE_IN,
                    in1=bq16[:, :].unsqueeze(2).to_broadcast([STK, GROUPS, T]),
                    op0=ALU.mult, op1=ALU.add).then_inc(q_read, 1)
                dve.wait_ge(q_read, 1)
                nc.vector.tensor_copy(qparts[:, :, :], qf[:, :, :]).then_inc(qsplit, 1)
                dve.wait_ge(qsplit, 2)
                nc.vector.tensor_tensor(qparts[half, :, :], qf[half, :, :], qparts[half, :, :],
                                        ALU.subtract).then_inc(qsplit, 1)
                dve.wait_ge(qsplit, 3)
                nc.vector.tensor_tensor(
                    qs[0:STK, 0, :].rearrange("p (a t) -> p a t", a=4),
                    qparts[:, 0, :].unsqueeze(1).to_broadcast([STK, 4, T]),
                    a_("maskq")[0:STK, :].unsqueeze(2).to_broadcast([STK, 4, T]), ALU.mult).then_inc(q0_done, 1)

            def low_keys(u):
                dve.wait_ge(act_done, u + 1)
                nc.vector.scalar_tensor_tensor(
                    out=kparts[:, 1, HALF * u:HALF * u + HALF], in0=ring[:, u % RING, 0:HALF], scalar=bk16[:, 0:1],
                    in1=kparts[:, 0, HALF * u:HALF * u + HALF], op0=ALU.add, op1=ALU.subtract).then_inc(klo_done, 1)

            def chunk_max(g, c, h, par):
                dve.wait_ge(p1_full, chunk_no(g, c, h) + 1)
                nc.vector.tensor_reduce(mx[:, par, h, c:c + 1], p1[:, h, :, 0:HALF], AX.XY,
                                        ALU.max).then_inc(p1_empty, 1)

            def group_max(g, par):
                dve.wait_ge(p1_empty, chunk_no(g, CHUNKS, 0))
                nc.vector.tensor_reduce(negmax[:, :], mx[:, par, :, :], AX.X, ALU.max,
                                        negate=True).then_inc(nm_raw, 1)
                dve.wait_ge(nm_raw, g + 1)
                nc.vector.tensor_scalar(negmax16[:, par, :], negmax[:, :], 1.0 / MSCALE, None,
                                        ALU.mult).then_inc(m_ready, 1)

            def save_sums(g):
                dve.wait_ge(probs_free, products_done(g))
                nc.vector.tensor_copy(accs[:, bass.ds(g, 1), :].rearrange("p g n -> p (g n)"),
                                      acc[:, 0:COLS]).then_inc(acc_free, 1)

            for u in range(2):
                low_keys(u)
            dve.wait_ge(xnT_ps, 1)
            nc.vector.tensor_copy(xnT[:, :], p1[:, 0, 0, 0:T]).then_inc(xnT_done, 1)
            for u in range(2, 4):
                low_keys(u)
            queries()
            for u in range(4, LEAD):
                low_keys(u)
            for c in range(CHUNKS):
                for h in range(2):
                    chunk_max(0, c, h, 0)
                    if 2 * c + h + LEAD < 2 * CHUNKS:
                        low_keys(2 * c + h + LEAD)
            group_max(0, 0)
            for h in range(2):
                chunk_max(1, 0, h, 1)
            dve.wait_ge(rel_ps, 1)
            nc.vector.tensor_copy(relT[:, :], acc[0:H, COLS:COLS + 2 * T - 1]).then_inc(rel_sb, 1)

            def lambda_dots():
                dve.wait_ge(b_in_s, 16)
                nc.vector.tensor_tensor(lamp[:, :, :].rearrange("p a b -> p (a b)"), b_("lamq", T), b_("lamk", T),
                                        ALU.mult).then_inc(lam_s, 1)
                dve.wait_ge(lam_s, 1)
                nc.vector.tensor_reduce(lamd[:, :], lamp[:, :, :], AX.X, ALU.add).then_inc(lam_s, 1)
                nc.vector.memset(coef[:, 0:1], 1.0 - LAMBDA_INIT).then_inc(coef_done, 1)
                nc.vector.tensor_tensor(xbo[:, :], a_("x")[0:T, :], b_("bo", T), ALU.add).then_inc(xbo_done, 1)

            def lambda_coefficients():
                dve.wait_ge(lam_e, 1)
                nc.vector.tensor_tensor(lamx[:, :], lame[:, 1:2], lame[:, 0:1], ALU.subtract).then_inc(lam_s, 1)
                dve.wait_ge(lam_s, 3)
                nc.vector.tensor_scalar(coef[:, 1:2], lamx[:, :], -LAMBDA_INIT, 1.0 - LAMBDA_INIT,
                                        ALU.add, ALU.mult).then_inc(coef_done, 1)
                dve.wait_ge(coef_done, 2)
                nc.vector.tensor_scalar(vsc[:, :], coef[:, 1:2], 1.0 - LAMBDA_INIT, None,
                                        ALU.add).then_inc(lam_s, 1)
                dve.wait_ge(lam_s, 4)
                nc.vector.tensor_scalar(vbt[:, :], b_("vb", T), vsc[:, 0:1], None, ALU.mult).then_inc(vbt_done, 1)

            def slot(g, par, last, last_but_one):
                for c in range(CHUNKS):
                    if c < CHUNKS - 1 and not last:
                        for h in range(2):
                            chunk_max(g + 1, c + 1, h, 1 - par)
                    elif not last:
                        group_max(g + 1, 1 - par)
                        if not last_but_one:
                            for h in range(2):
                                chunk_max(g + 2, 0, h, par)
                save_sums(g)

            with dve.Fori(0, (GROUPS - 2) // 2) as it:
                for par in range(2):
                    slot(2 * it + par, par, False, False)
            lambda_dots()
            slot(GROUPS - 2, 0, False, True)
            lambda_coefficients()
            slot(GROUPS - 1, 1, True, False)
            tail_dve(dve)

        @block.tensor
        def _(pe):
            def project_keys(u):
                if u % 2 == 0:
                    pe.wait_ge(ctx_in_s[u // 2], 16)
                if u >= RING:
                    pe.wait_ge(klo_done, u - RING + 1)
                pe.matmul(ring[:, u % RING, 0:HALF], wk16[:, :], ctxT[:, HALF * u:HALF * u + HALF],
                          start=True, stop=True).then_inc(lg_full, 1)

            def project_values(v):
                c, j = divmod(v, 2)
                i = 2 * CHUNKS + v
                if v < RING:
                    pe.wait_ge(klo_done, i - RING + 1)
                else:
                    pe.wait_ge(act_done, i - RING + 1)
                t0, nt = ((0, 4), (4, 3))[j]
                for t in range(nt):
                    k = P * (TPC * c + t0 + t)
                    last = pe.matmul(ring[:, i % RING, P * t:P * t + P], ctxT[:, k:k + P], b_("wv"),
                                     start=True, stop=True)
                last.then_inc(lg_full, 1)

            def pass1(g, c, h, par, arrived):
                if h == 0:
                    pe.wait_ge(kst_in[par][c], arrived)
                if not (isinstance(g, int) and chunk_no(g, c, h) < 2):
                    pe.wait_ge(p1_empty, chunk_no(g, c, h) - 1)
                q = qs[:, bass.ds(g, 1), T * 2 * h:T * 2 * h + 2 * T].rearrange("p g n -> p (g n)")
                for i in range(2):
                    k = CK * c + HALF * i
                    last = pe.matmul(p1[:, h, i, 0:HALF], q, kst[:, par, k:k + HALF], start=True, stop=True)
                last.then_inc(p1_full, 1)

            def pass2(g, c, e, par, last):
                k = EPC * c + e
                ahead_by = 5 if last else RING
                dst = last_logits(k) if last else ring[:, k % RING, :]
                if k >= ahead_by:
                    pe.wait_ge(act_done, entry_no(g, c, e) - ahead_by + 1)
                elif k >= RING:
                    pe.wait_ge(p1_empty, chunk_no(GROUPS, 0, 0))
                elif k == 0:
                    pe.wait_ge(act_done, entry_no(g, 0, 0))
                q = qs[:, bass.ds(g, 1), :].rearrange("p g n -> p (g n)")
                for i in range(ENTRY_TILES[e]):
                    t = TPC * c + ENTRY0[e] + i
                    done = pe.matmul(dst[:, COLS * i:COLS * i + COLS],
                                     kst[:, par, P * t:P * t + P], q, start=True, stop=True)
                done.then_inc(lg_full, 1)

            def values(g, c, par, it):
                if c == 0:
                    pe.wait_ge(v_in[par], 16 * it + 16)
                    pe.wait_ge(acc_free, g + 1)
                for e in range(EPC):
                    k = EPC * c + e
                    pe.wait_ge(act_done, entry_no(g, c, e + 1))
                    for i in range(ENTRY_TILES[e]):
                        t = TPC * c + ENTRY0[e] + i
                        j = BLK * (t % 4)
                        last = pe.matmul(acc[j:j + 2 * VW, 0:COLS], vcur[:, par, t, :],
                                         probs[:, (EPC * CHUNKS * par + k) % PROBS, COLS * i:COLS * i + COLS],
                                         start=(t < 4), stop=(t >= KT - 4))
                    last.then_inc(probs_free, 1)

            def max_row(g, par):
                pe.wait_ge(m_ready, g + 1)
                pe.wait_ge(act_done, entry_no(g - 1, CHUNKS, 0) - RING + 1)
                for h in range(2):
                    last = pe.matmul(ring[0:1, MROW % RING, P * h:P * h + P], negmax16[:, par, h:h + 1],
                                     ident16[:, :], start=True, stop=True)
                last.then_inc(lg_full, 1)

            pe.wait_ge(wk_done, 2)
            for u in range(3):
                project_keys(u)
            pe.wait_ge(xn_done, 1)
            pe.transpose(p1[:, 0, 0, 0:T], xn[:, :], ident[0:T, 0:T]).then_inc(xnT_ps, 1)
            project_keys(3)
            pe.wait_ge(wq_in, 16)
            pe.wait_ge(xnT_done, 1)
            for g in range(GROUPS):
                last = pe.matmul(p1[0:STK, 0, 1, T * g:T * g + T], a_("wq")[:, STK * g:STK * g + STK], xnT[:, :],
                                 start=True, stop=True)
            last.then_inc(q_ps, 1)
            for u in range(4, LEAD):
                project_keys(u)
            pe.wait_ge(q0_done, 1)
            pe.wait_ge(qs_zero, 1)
            pe.wait_ge(kst_set, 2)
            v = 0
            for c in range(CHUNKS):
                for h in range(2):
                    pass1(0, c, h, 0, 16)
                    u = 2 * c + h + LEAD
                    if u < 2 * CHUNKS:
                        project_keys(u)
                if u >= 2 * CHUNKS:
                    if v == 0:
                        pe.wait_ge(b_in_s, 16)
                    for _ in range(3):
                        if v < 2 * CHUNKS:
                            project_values(v)
                            v += 1
            pe.wait_ge(q_done, 1)
            for h in range(2):
                pass1(1, 0, h, 1, 16)
            while v < 2 * CHUNKS:
                project_values(v)
                v += 1
            pe.wait_ge(id16_done, 1)
            max_row(0, 0)
            pe.wait_ge(d_in_s, 16)
            pe.wait_ge(acc_free, 1)
            pe.matmul(acc[0:H, COLS:COLS + 2 * T - 1], d_("table", 32), d_("onehot", 32),
                      start=True, stop=True).then_inc(rel_ps, 1)
            pe.wait_ge(rel_sb, 1)

            def slot(g, par, it, last, last_but_one):
                for c in range(CHUNKS):
                    for h in range(2):
                        pass2(g, c, 2 * h, par, last)
                        pass2(g, c, 2 * h + 1, par, last)
                        if c < CHUNKS - 1 and not last:
                            pass1(g + 1, c + 1, h, 1 - par, stacked(it, par, 1))
                        elif not last and not last_but_one:
                            pass1(g + 2, 0, h, par, stacked(it, par, 2))
                    if c > 0:
                        values(g, c - 1, par, it)
                    if last:
                        sums(pe, c)
                if not last:
                    max_row(g + 1, 1 - par)
                values(g, CHUNKS - 1, par, it)

            with pe.Fori(0, (GROUPS - 2) // 2) as it:
                for par in range(2):
                    slot(2 * it + par, par, it, False, False)
            slot(GROUPS - 2, 0, (GROUPS - 2) // 2, False, True)
            slot(GROUPS - 1, 1, (GROUPS - 2) // 2, True, False)
            tail_pe(pe)


def _buckets():
    half, exact, far = 16, 8, 128
    out = []
    for d in range(1 - T, T):
        n = abs(d)
        large = exact + int(np.float32(np.log(np.float32(max(n, 1)) / np.float32(exact)))
                            / np.float32(np.log(far / exact)) * np.float32(half - exact))
        out.append((half if d > 0 else 0) + (n if n < exact else min(large, half - 1)))
    return out


def _pack(cols, total, rows, parts):
    a = np.zeros((rows, total), np.float32)
    for k, v in parts.items():
        a[0:v.shape[0], cols[k][0]:cols[k][1]] = v
    return a


def kernel(**inputs):
    import concourse.bacc as _bacc
    from concourse.bass_utils import run_bass_kernel_spmd as _run

    i = {k: np.asarray(v) for k, v in inputs.items()}
    L = "L0_"
    inw, inb = i[L + "xattn_in_proj_weight"].T, i[L + "xattn_in_proj_bias"]
    r = np.arange(P)
    row = np.arange(STK) % (2 * GD) // 2
    maskq = (row[:, None] // SUB == np.arange(4)[None, :])
    dims = GD * np.arange(GROUPS)[:, None] + row[None, :]
    sel = np.zeros((P, 2 * VW), np.float32)
    for j in range(4):
        sel[BLK * j + np.arange(2 * VW), np.arange(2 * VW)] = 1
    maskk = (r[:, None] // HD % (H // 2) == np.arange(H // 2)[None, :])
    tri = np.broadcast_to((np.arange(E)[None, :] < np.arange(E)[:, None]).reshape(1, E * E), (P, E * E))
    onehot = (np.arange(32)[:, None] == np.array(_buckets())[None, :])
    a = _pack(A_AT, A_N, P, dict(x=i["x"][0], ident=np.eye(P), bk=inb[D:2 * D, None], bq=inb[0:D][dims.T],
                                 maskq=maskq, wk=inw[:, D:2 * D], wq=inw[:, 0:D][:, dims.ravel()]))
    b = _pack(B_AT, B_N, P, dict(
        wv=inw[:, 2 * D:3 * D], sel=sel, vb=np.broadcast_to(inb[2 * D:], (T, D)),
        bo=np.broadcast_to(i[L + "xattn_out_proj_bias"], (T, D)),
        lamq=np.broadcast_to(np.concatenate([i[L + "xattn_lambda_q1"], i[L + "xattn_lambda_q2"]]), (T, 2 * SUB)),
        lamk=np.broadcast_to(np.concatenate([i[L + "xattn_lambda_k1"], i[L + "xattn_lambda_k2"]]), (T, 2 * SUB)),
        wo=i[L + "xattn_out_proj_weight"].T, awq=i[L + "attn_w_q"].T, awk=i[L + "attn_w_k"].T,
        awv=i[L + "attn_w_v"].T, awo=i[L + "attn_w_o"].T, maskk=maskk, tri=tri,
        rw2=i[L + "ffn_rw2"].reshape(FC, P, E).transpose(1, 0, 2).reshape(P, FC * E), flip=np.kron(np.eye(2), np.eye(T)[::-1])))
    eb1 = i[L + "ffn_eb1"].reshape(4, 2 * FC, P)
    d = _pack(D_AT, D_N, 32, dict(
        table=i[L + "attn_rel_bias_table"], onehot=onehot, blk=WSCALE * np.repeat(np.eye(E), T, axis=1),
        blk2=WSCALE ** 2 * np.repeat(np.eye(E), T, axis=1), rb1=i[L + "ffn_rb1"].reshape(FC, P),
        eb1=eb1.transpose(1, 0, 2).reshape(2 * FC, 4 * P), eb2=i[L + "ffn_eb2"],
        ones=np.ones((1, P)), rb2=i[L + "ffn_rb2"].reshape(1, E)))
    arrays = dict(
        a_in=a, ctx_in=i["ctx_1024"][0].T, b_in=b,
        w1_in=np.concatenate([i[L + "ffn_rw1"], i[L + "ffn_ew1"].transpose(1, 0, 2).reshape(P, E * FH)], axis=1),
        w2_in=i[L + "ffn_ew2"].reshape(E, FC, P, D).transpose(2, 0, 1, 3).reshape(P, N2), d_in=d)
    arrays = {k: np.ascontiguousarray(v) for k, v in arrays.items()}
    nc = _bacc.Bacc("TRN2", target_bir_lowering=False, num_devices=1)
    args = [nc.dram_tensor(k, v.shape, F32, kind="ExternalInput").ap() for k, v in arrays.items()]
    scratch = nc.dram_tensor("relative_bias", (H, 2 * T - 1), F32, kind="Internal").ap()
    kparts = nc.dram_tensor("key_parts", (D, 2, S), F16, kind="Internal").ap()
    out = nc.dram_tensor("out_dram", (T, D), F32, kind="ExternalOutput").ap()
    perceiver_layer(nc, *args, scratch, kparts, out)
    got = _run(nc, [arrays], core_ids=[0])
    return got.results[0]["out_dram"].reshape(1, T, D)
```

```python
from contextlib import ExitStack

import numpy as np

import concourse.bass as bass
from concourse import mybir

F32 = mybir.dt.float32
F16 = mybir.dt.float16
U32 = mybir.dt.uint32
ALU = mybir.AluOpType
ACT = mybir.ActivationFunctionType
AX = mybir.AxisListType

P = 128
T = 64
S = 6272
D = 128
H = 16
HD = D // H
SUB = HD // 2
GROUPS = H // 2
GD = 2 * HD
BLK = 32
STK = 4 * GD
CHUNKS = 7
CK = S // CHUNKS
HALF = CK // 2
KT = S // P
TPC = KT // CHUNKS
ENTRY_TILES = [2, 2, 2, 1]
ENTRY0 = [0, 2, 4, 6]
EPC = len(ENTRY_TILES)
COLS = 2 * 2 * T
PER_SLOT = EPC * CHUNKS + 1
MROW = EPC * CHUNKS
RING = 3
PROBS = 14
VW = HD + 1
SCALE_IN = 16.0
MSCALE = SCALE_IN * SCALE_IN
MPAIR = float(np.array([MSCALE, MSCALE], np.float16).view(np.float32)[0])
EPS = 1e-5
LAMBDA_INIT = 0.8 - 0.6
E = 8
FH = 512
FC = FH // P
WSCALE = 16.0
N1 = FH + E * FH
N2 = E * FC * D
STAGE = 1024
N_BIAS = 6 * P
VALUE_TILES = [range(40, 49), range(0, 4), range(4, 8), range(8, 16), range(16, 24), range(24, 32), range(32, 40)]
ORDER = [("k", u) for u in range(8)] + [(x[0], int(x[1:])) for x in (
    "v0 k8 v1 m0 k9 k10 m1 v2 k11 m2 v3 k12 m3 v4 k13 v5 m4 v6 v7 m5 v8 v9 v10 m6 v11 v12 v13").split()]
UNITS = [x for x in ORDER if x[0] != "m"]
WIDE = ORDER.index(("m", 0)) - 2
UNIT_BANK = []
for n in range(len(UNITS)):
    UNIT_BANK.append(min((2, 3, 4, 5, 6) if n < WIDE else (4, 5, 6),
                         key=lambda b: max([m for m in range(n) if UNIT_BANK[m] == b], default=-1)))
IDLE = (7, 4, 6, 4, 7, 18, 2, 3)
WARM = 9

A_COLS = dict(x=D, ident=P, bk=1, bq=GROUPS, maskq=4, wk=D, wv=D, wq=GROUPS * STK)
A_FIRST = A_COLS["x"] + A_COLS["ident"] + 1 + GROUPS + 4
B_COLS = dict(sel=2 * VW, vb=1, bo=D, lamq=2 * SUB, lamk=2 * SUB, wo=D, awq=D, awk=D, awv=D, awo=2 * D,
              maskk=H // 2, maskh=2, tri=E * E, flip=P, rw2=FC * E, ident2=T)
D_COLS = dict(table=H, onehot=2 * T - 1, spread=E * T, biases=N_BIAS, ones=P, rb2=E)


def offsets(cols):
    out, at = {}, 0
    for k, n in cols.items():
        out[k] = (at, at + n)
        at += n
    return out, at


A_AT, A_N = offsets(A_COLS)
B_AT, B_N = offsets(B_COLS)
D_AT, D_N = offsets(D_COLS)


def perceiver_layer(nc, a_in, ctx_in, b_in, w1_in, w2_in, d_in, bias_scratch, kparts_dram, out):
    with ExitStack() as ctx:
        def sb(name, shape, dt=F32):
            return ctx.enter_context(nc.sbuf_tensor(name, shape, dt))

        def sem(name):
            return ctx.enter_context(nc.semaphore(name))

        wa = sb("wa", [P, A_N])
        wb = sb("wb", [P, B_N])
        wd = sb("wd", [2 * BLK, D_N])
        bscaled = sb("bscaled", [2 * BLK, N_BIAS])
        bparts = sb("bparts", [P, N_BIAS], F16)
        spread16 = sb("spread16", [P, E * T], F16)
        ctxT = sb("ctxT", [P, S])
        kparts = sb("kparts", [P, 2, S], F16)
        kst = sb("kst", [P, 2, S], F16)
        qs = sb("qs", [P, GROUPS, COLS], F16)
        vall = sb("vall", [P, GROUPS, KT, 2 * VW])
        vcur = sb("vcur", [P, 2, KT, 2 * VW])
        probs = sb("probs", [P, PROBS, 2 * COLS])
        accs = sb("accs", [P, GROUPS, COLS])
        w1p = kparts[:, :, :].rearrange("p a n -> p (a n)")[:, 0:2 * N1].rearrange("p (a n) -> p a n", a=2)
        w2p = ctxT[:, 0:N2].bitcast(F16).rearrange("p (a n) -> p a n", a=2)
        stage = ctxT[:, N2:N2 + 2 * STAGE].rearrange("p (a n) -> p a n", a=2)
        warm = sb("warm", [P, 512], F16)
        ident16 = sb("ident16", [P, P], F16)
        wk16 = sb("wk16", [P, D])
        bk16 = sb("bk16", [P, 1])
        stats = sb("stats", [T, 6])
        mv = sb("mv", [T, 2])
        rstd = sb("rstd", [T, 1])
        veps = sb("veps", [T, 1])
        power = sb("power", [T, 1])
        xn = sb("xn", [T, D])
        xnT = sb("xnT", [P, T])
        bq16 = sb("bq16", [STK, GROUPS])
        qf = sb("qf", [STK, GROUPS, T])
        qparts = sb("qparts", [STK, GROUPS, T], F16)
        mx = sb("mx", [P, 2, 2, CHUNKS])
        negmax = sb("negmax", [P, 2])
        negmax16 = sb("negmax16", [P, 2, 2], F16)
        lamp = sb("lamp", [P, 2, SUB])
        lamd = sb("lamd", [P, 2])
        lame = sb("lame", [P, 2])
        lamx = sb("lamx", [P, 1])
        spare = sb("spare", [1, 1])
        spare2 = sb("spare2", [1, 1])
        coef = sb("coef", [P, 1])
        coef2 = sb("coef2", [P, 1])
        vbt = sb("vbt", [P, 1])
        xbo = sb("xbo", [T, D])
        rec = sb("rec", [P, H])
        o2 = sb("o2", [P, H, HD])
        attnT = sb("attnT", [P, T])
        x1 = sb("x1", [T, D])
        x1T = sb("x1T", [P, 2, T])
        qTs = sb("qTs", [P, 2, T])
        kbd = sb("kbd", [P, H // 2, T])
        vbd = sb("vbd", [P, H // 2, BLK])
        relT = sb("relT", [H, 2 * T - 1])
        relb = sb("relb", [P, H // 2, T])
        smx = sb("smx", [P, H // 2])
        ssub = sb("ssub", [P, H // 2, T])
        sexp = sb("sexp", [P, H // 2, T])
        pT = sb("pT", [P, 4, 2, T])
        ssum = sb("ssum", [P, H // 2])
        rec2 = sb("rec2", [P, H // 2])
        rspread = sb("rspread", [P, 4, BLK // HD, HD])
        recT = sb("recT", [P, 2, T])
        attn2 = sb("attn2", [P, 2, T])
        x2 = sb("x2", [T, D])
        x2T = sb("x2T", [P, 2, T], F16)
        hr = sb("hr", [P, FC, T])
        lg = sb("lg", [T, E])
        gt = sb("gt", [T, E, E])
        eq = sb("eq", [T, E, E])
        eqt = sb("eqt", [T, E, E])
        ahead = sb("ahead", [T, E, E])
        rank = sb("rank", [T, E])
        lmx = sb("lmx", [T, 1])
        lsub = sb("lsub", [T, E])
        lexp = sb("lexp", [T, E])
        sel2 = sb("sel2", [T, E])
        den = sb("den", [T, 1])
        rden = sb("rden", [T, 1])
        gdiag = sb("gdiag", [T, E, T])
        gall = ssub
        unscale = sb("unscale", [T, P])
        hs = sb("hs", [P, 4, 2, 8 * T], F16)
        gated = kbd
        ysum = sb("ysum", [P, 2, T])
        y = sb("y", [T, D])

        def a_(k):
            return wa[:, A_AT[k][0]:A_AT[k][1]]

        def b_(k, n=P):
            return wb[0:n, B_AT[k][0]:B_AT[k][1]]

        def d_(k, n):
            return wd[0:n, D_AT[k][0]:D_AT[k][1]]

        ident = a_("ident")

        p1 = ctx.enter_context(nc.psum_tensor("p1", [P, 2, 2, 512], F32))
        ring = ctx.enter_context(nc.psum_tensor("ring", [P, RING, 512], F32))
        acc = ctx.enter_context(nc.psum_tensor("acc", [P, 512], F32))

        a_in_s = sem("a_loaded")
        b_in_s = sem("b_loaded")
        d_in_s = sem("d_loaded")
        w_in = [sem(f"weights_staged{n}") for n in range(2)]
        w_scaled = sem("weights_scaled")
        w_high = sem("weights_high_part")
        w_split = sem("weights_split")
        unscale_set = sem("unscale_set")
        table_in = sem("spare_set")
        warm_set = sem("warm_set")
        ctx_in_s = [sem(f"ctx_loaded{c}") for c in range(CHUNKS)]
        kst_in = [[sem(f"keys_stacked{p}_{c}") for c in range(CHUNKS)] for p in range(2)]
        k_out = [sem(f"keys_spread{c}") for c in range(CHUNKS)]
        wk_in = sem("wk_loaded")
        wq_in = sem("wq_loaded")
        v_in = [sem(f"values_in{p}") for p in range(2)]
        qs_zero = sem("qs_zeroed")
        kst_set = sem("kst_row_set")
        ones_set = sem("ones_set")
        ln_s = sem("ln_steps")
        power_set = sem("power_set")
        xn_done = sem("xn_done")
        xnT_ps = sem("xnT_in_psum")
        xnT_done = sem("xnT_done")
        q_ps = sem("q_in_psum")
        id16_done = sem("ident16_done")
        wk_done = sem("wk_scaled")
        q_read = sem("q_out_of_psum")
        qsplit = sem("q_split_steps")
        q0_done = sem("queries0_done")
        q_done = sem("queries_done")
        klo_done = sem("klo_done")
        p1_full = sem("pass1_full")
        p1_empty = sem("pass1_reduced")
        nm_raw = sem("negmax_done")
        m_ready = sem("negmax16_ready")
        lg_full = sem("logits_full")
        act_done = sem("ring_entry_read")
        probs_free = sem("probs_free")
        acc_free = sem("sums_bank_free")
        lam_s = sem("lambda_steps")
        lam_e = sem("lambda_exp")
        coef_done = sem("coef_done")
        vbt_done = sem("vbt_done")
        xbo_done = sem("xbo_done")
        vbd_zero = sem("vbd_zeroed")
        po_ps = sem("attention_sums_in_psum")
        norm_s = sem("normalise_steps")
        attn_done = sem("attn_done")
        attnT_ps = sem("attnT_in_psum")
        attnT_done = sem("attnT_done")
        proj1_ps = sem("cross_attention_in_psum")
        x1_done = sem("x1_done")
        qk_ps = sem("self_qk_in_psum")
        v_ps = sem("self_v_in_psum")
        qT_done = sem("self_q_halves_done")
        pT0_done = sem("self_probsT_first_half")
        pT1_done = sem("self_probsT_second_half")
        qk_done = sem("self_qk_done")
        vbd_done = sem("self_v_done")
        sc_ps = sem("self_scores_in_psum")
        smx_done = sem("self_max_done")
        ssub_done = sem("self_shifted")
        sexp_done = sem("self_exp_done")
        pT_ps = sem("self_probsT_in_psum")
        pv_ps = sem("self_values_in_psum")
        ssum_done = sem("self_sums_done")
        rspread_zero = sem("reciprocals_zeroed")
        rspread_done = sem("self_reciprocals_spread")
        recT_ps = sem("self_reciprocalsT_in_psum")
        recT_done = sem("self_reciprocalsT_done")
        bias_s = sem("bias_steps")
        biases_split = sem("biases_split")
        rec2_done = sem("self_reciprocal_done")
        attn2_done = sem("self_attn_done")
        proj2_ps = sem("self_attention_in_psum")
        x2_done = sem("x2_done")
        hr_ps = sem("router_hidden_in_psum")
        hr_done = sem("router_hidden_done")
        lg_ps = sem("router_logits_in_psum")
        gate_s = sem("gate_steps")
        lexp_done = sem("router_exp_done")
        he_ps = sem("expert_hidden_in_psum")
        hs_done = sem("expert_hidden_done")
        eo_ps = sem("expert_out_in_psum")
        hl_done = sem("expert_hidden_low_done")
        gdiag_done = sem("gates_spread")
        gall_ps = sem("gates_in_psum")
        gall_done = sem("gates_on_all_partitions")
        gated_done = sem("gated_done")
        ysum_done = sem("mixture_summed")
        y_ps = sem("mixture_in_psum")
        y_done = sem("y_done")
        out_done = sem("out_written")
        rel_ps = sem("rel_in_psum")
        rel_sb = sem("rel_in_sbuf")
        rel_out = sem("rel_in_dram")
        rel_in = sem("rel_spread")

        block = ctx.enter_context(nc.Block())

        def chunk_no(g, c, h):
            return 2 * CHUNKS * g + 2 * c + h

        def entry_no(g, c, e):
            return PER_SLOT * (g + 1) + EPC * c + e

        def products_done(g):
            return PROBS + EPC * CHUNKS * (g + 1)

        def stacked(it, par, ahead_by):
            return (it + (par + ahead_by) // 2 + 1) * 16 + 16 * ((par + ahead_by + 1) % 2)

        def bank(i):
            return p1[:, i // 2, i % 2, :] if i < 4 else ring[:, i - 4, :] if i < 7 else acc[:, :]

        po = bank(0)[:, 0:H * VW].rearrange("p (h v) -> p h v", h=H)
        x1_ps = bank(7)[0:T, 0:D]
        x2_ps = bank(4)[0:T, 2 * D:3 * D]
        y_bank = bank(5)[0:T, D:2 * D]
        sc = bank(6).rearrange("p (h k) -> p h k", h=H // 2)
        SPLITS = [(p, n, min(n + STAGE, total)) for p, total in enumerate((N1, N2)) for n in range(0, total, STAGE)]
        ALL_READ = PER_SLOT * (GROUPS + 1) - 1

        def unit_read(engine, i):
            kind, u = UNITS[i]
            if kind == "k":
                engine.wait_ge(klo_done, u + 1)
            else:
                engine.wait_ge(act_done, i + 1)

        def value_tiles(v):
            return TPC * (v // 2) + 4 * (v % 2), 4 - v % 2

        def last_logits(k):
            return bank((4, 5, 6, 2, 3)[k % 5])

        def sums(pe, g):
            pe.wait_ge(acc_free, g + 2)
            for h in range(2):
                i = 2 * g + h
                last = pe.matmul(bank(0)[:, VW * i:VW * i + VW], accs[:, g, 2 * T * h:2 * T * h + 2 * T],
                                 b_("sel")[:, VW * h:VW * h + VW], start=True, stop=True)
            return last

        def mixture_bias(pe, out, k, n0, n, start=True):
            pe.matmul(out[:, n0:n0 + n], bparts[:, P * k:P * k + P], spread16[:, n0:n0 + n], start=start, stop=False,
                      skip_group_check=True)

        def keep_clock(pe, n):
            for _ in range(n):
                pe.matmul(bank(3)[:, 0:P], warm[:, 0:P], warm[:, 0:P], start=True, stop=True)

        def add_to_bank(pe, out, x):
            pe.matmul(out, ident[0:T, 0:T], x, start=True, stop=False, skip_group_check=True)

        def split_products(pe, out, w, x):
            for wn in range(2):
                for xn_ in range(2):
                    last = pe.matmul(out, w(wn), x(xn_), start=False, stop=True, skip_group_check=True)
            return last

        def tail_pe(pe):
            sums(pe, GROUPS - 1).then_inc(po_ps, 1)
            pe.wait_ge(xbo_done, 1)
            add_to_bank(pe, x1_ps, xbo[:, :])
            keep_clock(pe, IDLE[0])
            pe.wait_ge(attn_done, 1)
            pe.matmul(bank(5)[:, 0:T], o2[:, :, :].rearrange("p h v -> p (h v)"), b_("ident2"), start=True,
                      stop=True).then_inc(attnT_ps, 1)
            keep_clock(pe, IDLE[1])
            pe.wait_ge(attnT_done, 1)
            pe.matmul(x1_ps, attnT[:, :], b_("wo"), start=False, stop=True, skip_group_check=True).then_inc(proj1_ps, 1)
            pe.wait_ge(act_done, ALL_READ)
            pe.wait_ge(rel_in, 32)
            pe.matmul(bank(6), b_("flip"), relb[:, :, :].rearrange("p h k -> p (h k)"), start=True, stop=False,
                      skip_group_check=True)
            keep_clock(pe, IDLE[2])
            pe.wait_ge(xn_done, 2)
            pe.transpose(bank(5)[:, 0:T], xn[:, :], ident[0:T, 0:T]).then_inc(xnT_ps, 1)
            keep_clock(pe, IDLE[3])
            pe.wait_ge(xnT_done, 2)
            pe.matmul(bank(4)[:, 0:T], b_("awq"), x1T[:, 0, :], start=True, stop=True)
            pe.matmul(bank(2)[:, 0:T], b_("awk"), x1T[:, 0, :], start=True, stop=True).then_inc(qk_ps, 1)
            pe.wait_ge(x1_done, 1)
            pe.matmul(bank(7)[:, 0:D], x1T[:, :, :].rearrange("p a t -> p (a t)"), b_("awv"),
                      start=True, stop=True).then_inc(v_ps, 1)
            keep_clock(pe, IDLE[4])
            pe.wait_ge(qk_done, 1)
            pe.wait_ge(qT_done, 2)
            pe.matmul(bank(6), qTs[:, :, :].rearrange("p a t -> p (a t)"), kbd[:, :, :].rearrange("p h k -> p (h k)"),
                      start=False, stop=True, skip_group_check=True).then_inc(sc_ps, 1)
            add_to_bank(pe, x2_ps, x1[:, :])
            keep_clock(pe, IDLE[5])
            for n in range(4):
                if n % 2 == 0:
                    pe.wait_ge(sexp_done, n // 2 + 1)
                if n == 2:
                    pe.wait_ge(vbd_done, 2)
                last = pe.transpose(bank(5 + 2 * (n // 2))[:, P * (n % 2):P * (n % 2) + P],
                                    sexp[:, 2 * n:2 * n + 2, :].rearrange("p h k -> p (h k)"), ident)
                if n % 2 == 1:
                    last.then_inc(pT_ps, 1)
            keep_clock(pe, IDLE[6])
            for m in range(4):
                if m % 2 == 0:
                    pe.wait_ge((pT0_done, pT1_done)[m // 2], 1)
                for half in range(2):
                    last = pe.matmul(bank(4)[BLK * m:BLK * m + BLK, T * half:T * half + T], vbd[:, 4 * half + m, :],
                                     pT[:, m, half, :], start=(m >= 2 and half == 0), stop=True,
                                     skip_group_check=True)
            last.then_inc(pv_ps, 1)
            pe.wait_ge(rspread_done, 1)
            pe.transpose(bank(2)[:, 0:2 * T], rspread[:, :, :, :].rearrange("p m h v -> p (m h v)"),
                         ident).then_inc(recT_ps, 1)
            keep_clock(pe, IDLE[7])
            pe.wait_ge(attn2_done, 1)
            for half in range(2):
                last = pe.matmul(x2_ps, attn2[:, half, :], b_("awo")[:, D * half:D * half + D], start=False,
                                 stop=(half == 1), skip_group_check=True)
            last.then_inc(proj2_ps, 1)
            pe.wait_ge(biases_split, 1)
            mixture_bias(pe, bank(6), 4, 0, FC * T)
            for b in range(4):
                mixture_bias(pe, bank(b), b, 0, 8 * T)
            mixture_bias(pe, bank(7), 5, 0, E // 2 * T)
            mixture_bias(pe, bank(6), 5, E // 2 * T, E // 2 * T, start=False)
            pe.wait_ge(xn_done, 3)
            pe.transpose(bank(4)[:, 0:T], xn[:, :], ident[0:T, 0:T]).then_inc(xnT_ps, 1)
            pe.wait_ge(x2_done, 1)
            add_to_bank(pe, y_bank, x2[:, :])
            pe.wait_ge(w_split, len(SPLITS))
            pe.wait_ge(xnT_done, 4)
            for f in range(FC):
                last = split_products(pe, bank(6)[:, T * f:T * f + T],
                                      lambda n: w1p[:, n, P * f:P * f + P], lambda n: x2T[:, n, :])
            last.then_inc(hr_ps, 1)

            def expert_hidden(b):
                for n in range(8):
                    k = FH + (8 * b + n) * P
                    last = split_products(pe, bank(b)[:, T * n:T * n + T],
                                          lambda m: w1p[:, m, k:k + P], lambda m: x2T[:, m, :])
                last.then_inc(he_ps, 1)

            def expert_out(b):
                pe.wait_ge(hl_done, b + 1)
                for n in range(8):
                    e, f = 2 * b + n // FC, n % FC
                    k = (e * FC + f) * D
                    last = split_products(pe, bank(7 if e < E // 2 else 6)[:, T * e:T * e + T],
                                          lambda m: w2p[:, m, k:k + D], lambda m: hs[:, b, m, T * n:T * n + T])
                return last

            expert_hidden(0)
            pe.wait_ge(hr_done, 1)
            pe.matmul(bank(5)[0:T, 0:E], d_("ones", 1)[:, 0:T], d_("rb2", 1), start=False, stop=False,
                      skip_group_check=True)
            for f in range(FC):
                last = pe.matmul(bank(5)[0:T, 0:E], hr[:, f, :], b_("rw2")[:, E * f:E * f + E],
                                 start=False, stop=(f == FC - 1), skip_group_check=True)
            last.then_inc(lg_ps, 1)
            for b in range(1, 4):
                expert_hidden(b)
            expert_out(0)
            expert_out(1).then_inc(eo_ps, 1)
            pe.wait_ge(gdiag_done, 1)
            pe.wait_ge(unscale_set, 1)
            pe.matmul(bank(4), unscale[:, :], gdiag[:, :, :].rearrange("p e t -> p (e t)"), start=True,
                      stop=True).then_inc(gall_ps, 1)
            expert_out(2)
            expert_out(3).then_inc(eo_ps, 1)
            for half in range(2):
                pe.wait_ge(ysum_done, half + 1)
                last = pe.matmul(y_bank, ysum[:, half, :], ident, start=False, stop=(half == 1), skip_group_check=True)
            last.then_inc(y_ps, 1)

        def tail_act(act):
            act.wait_ge(ln_s, 4 + 1)
            nc.scalar.copy(x1[:, :], x1_ps).then_inc(x1_done, 1)
            act.wait_ge(qk_ps, 1)
            for half in range(2):
                nc.scalar.activation(qTs[:, half, :], bank(4)[:, 0:T], ACT.Copy,
                                     scale=b_("maskh")[:, half:half + 1]).then_inc(qT_done, 1)
            act.wait_ge(vbd_zero, 1)
            act.wait_ge(v_ps, 1)
            for h2 in range(2):
                r = T * h2
                nc.scalar.copy(vbd[r:r + T, :, HD * h2:HD * h2 + HD],
                               bank(7)[r:r + T, 0:D].rearrange("p (n h v) -> p n h v", h=2, v=HD)[:, :, h2, :]
                               ).then_inc(vbd_done, 1)
            for n in range(2):
                act.wait_ge(ssub_done, n + 1)
                nc.scalar.activation(sexp[:, 4 * n:4 * n + 4, :], ssub[:, 4 * n:4 * n + 4, :],
                                     ACT.Exp).then_inc(sexp_done, 1)
            act.wait_ge(pT_ps, 2)
            nc.scalar.copy(pT[:, 2:4, :, :].rearrange("p a b t -> p (a b t)"),
                           bank(7)[:, 0:2 * P]).then_inc(pT1_done, 1)
            act.wait_ge(recT_ps, 1)
            nc.scalar.copy(recT[:, :, :].rearrange("p a t -> p (a t)"), bank(2)[:, 0:2 * T]).then_inc(recT_done, 1)
            act.wait_ge(ln_s, 8 + 1)
            nc.scalar.copy(x2[:, :], x2_ps).then_inc(x2_done, 1)
            act.wait_ge(hr_ps, 1)
            nc.scalar.activation(hr[:, :, :].rearrange("p f t -> p (f t)"), bank(6)[:, 0:FC * T], ACT.Relu,
                                 scale=1.0 / WSCALE).then_inc(hr_done, 1)
            for b in range(4):
                act.wait_ge(he_ps, b + 1)
                nc.scalar.activation(hs[:, b, 0, :], bank(b), ACT.Relu).then_inc(hs_done, 1)
                if b == 1:
                    act.wait_ge(gate_s, 3)
                    nc.scalar.activation(lexp[:, :], lsub[:, :], ACT.Exp).then_inc(lexp_done, 1)
            act.wait_ge(gall_ps, 1)
            nc.scalar.copy(gall[:, :, :].rearrange("p e t -> p (e t)"), bank(4)).then_inc(gall_done, 1)

        def deviation(pool, n):
            pool.wait_ge(ln_s, 4 * n + 3)
            nc.gpsimd.tensor_tensor(rstd[:, :], veps[:, :], power[:, :], ALU.pow).then_inc(ln_s, 1)

        def layer_norm(dve, x_ps, x, x_done, n):
            nc.vector.bn_stats(stats[:, :], x_ps).then_inc(ln_s, 1)
            dve.wait_ge(ln_s, 4 * n + 1)
            nc.vector.bn_aggr(mv[:, :], stats[:, :]).then_inc(ln_s, 1)
            dve.wait_ge(ln_s, 4 * n + 2)
            nc.vector.tensor_scalar(veps[:, :], mv[:, 1:2], EPS, None, ALU.add).then_inc(ln_s, 1)
            dve.wait_ge(x_done, 1)
            dve.wait_ge(ln_s, 4 * n + 4)
            nc.vector.tensor_scalar(xn[:, :], x, mv[:, 0:1], rstd[:, 0:1],
                                    ALU.subtract, ALU.mult).then_inc(xn_done, 1)

        def tail_dve(dve):
            dve.wait_ge(po_ps, 1)
            nc.vector.reciprocal(rec[:, :], po[:, :, HD]).then_inc(norm_s, 1)
            dve.wait_ge(norm_s, 1)
            dve.wait_ge(coef_done, 2)
            nc.vector.scalar_tensor_tensor(out=o2[:, :, :], in0=po[:, :, 0:HD], scalar=coef[:, 0:1],
                                           in1=rec[:, :].unsqueeze(2).to_broadcast([P, H, HD]),
                                           op0=ALU.mult, op1=ALU.mult).then_inc(attn_done, 1)
            dve.wait_ge(attnT_ps, 1)
            nc.vector.tensor_scalar(attnT[:, :], bank(5)[:, 0:T], vbt[:, 0:1], None, ALU.add).then_inc(attnT_done, 1)
            dve.wait_ge(proj1_ps, 1)
            layer_norm(dve, x1_ps, x1[:, :], x1_done, 1)
            dve.wait_ge(xnT_ps, 2)
            nc.vector.tensor_copy(x1T[:, :, :],
                                  bank(5)[:, 0:T].unsqueeze(1).to_broadcast([P, 2, T])).then_inc(xnT_done, 1)
            dve.wait_ge(qk_ps, 1)
            nc.vector.tensor_tensor(kbd[:, :, :], bank(2)[:, 0:T].unsqueeze(1).to_broadcast([P, H // 2, T]),
                                    b_("maskk").unsqueeze(2).to_broadcast([P, H // 2, T]), ALU.mult).then_inc(qk_done, 1)
            dve.wait_ge(sc_ps, 1)
            nc.vector.tensor_reduce(smx[:, :], sc, AX.X, ALU.max).then_inc(smx_done, 1)
            dve.wait_ge(smx_done, 1)
            for n in range(2):
                heads = slice(4 * n, 4 * n + 4)
                nc.vector.tensor_tensor(ssub[:, heads, :], sc[:, heads, :],
                                        smx[:, heads].unsqueeze(2).to_broadcast([P, 4, T]),
                                        ALU.subtract).then_inc(ssub_done, 1)
            for n in range(2):
                dve.wait_ge(sexp_done, n + 1)
                nc.vector.tensor_reduce(ssum[:, 4 * n:4 * n + 4], sexp[:, 4 * n:4 * n + 4, :], AX.X,
                                        ALU.add).then_inc(ssum_done, 1)
                if n == 0:
                    dve.wait_ge(pT_ps, 1)
                    nc.vector.tensor_copy(pT[:, 0:2, :, :].rearrange("p a b t -> p (a b t)"),
                                          bank(5)[:, 0:2 * P]).then_inc(pT0_done, 1)
            dve.wait_ge(ssum_done, 2)
            nc.vector.reciprocal(rec2[:, :], ssum[:, :]).then_inc(rec2_done, 1)
            dve.wait_ge(rec2_done, 1)
            dve.wait_ge(rspread_zero, 1)
            nc.vector.tensor_copy(rspread[:, :, 0:2, :], rec2[:, :].rearrange("p (m h) -> p m h", h=2)
                                  .unsqueeze(3).to_broadcast([P, 4, 2, HD])).then_inc(rspread_done, 1)
            dve.wait_ge(pv_ps, 1)
            dve.wait_ge(recT_done, 1)
            nc.vector.tensor_tensor(attn2[:, :, :].rearrange("p a t -> p (a t)"), bank(4)[:, 0:2 * T],
                                    recT[:, :, :].rearrange("p a t -> p (a t)"), ALU.mult).then_inc(attn2_done, 1)
            dve.wait_ge(proj2_ps, 1)
            layer_norm(dve, x2_ps, x2[:, :], x2_done, 2)
            dve.wait_ge(xnT_ps, 3)
            nc.vector.tensor_copy(x2T[:, 0, :], bank(4)[:, 0:T]).then_inc(xnT_done, 1)
            dve.wait_ge(xnT_done, 3)
            nc.vector.tensor_tensor(x2T[:, 1, :], bank(4)[:, 0:T], x2T[:, 0, :], ALU.subtract).then_inc(xnT_done, 1)

            def low_hidden(b):
                dve.wait_ge(hs_done, b + 1)
                nc.vector.scalar_tensor_tensor(out=hs[:, b, 1, :], in0=bank(b), scalar=0.0, in1=hs[:, b, 0, :],
                                               op0=ALU.max, op1=ALU.subtract).then_inc(hl_done, 1)

            dve.wait_ge(lg_ps, 1)
            nc.vector.tensor_copy(lg[:, :], bank(5)[0:T, 0:E]).then_inc(gate_s, 1)
            dve.wait_ge(gate_s, 1)
            nc.vector.tensor_reduce(lmx[:, :], lg[:, :], AX.X, ALU.max).then_inc(gate_s, 1)
            dve.wait_ge(gate_s, 2)
            nc.vector.tensor_scalar(lsub[:, :], lg[:, :], lmx[:, 0:1], None, ALU.subtract).then_inc(gate_s, 1)
            other = lg[:, :].unsqueeze(1).to_broadcast([T, E, E])
            own = lg[:, :].unsqueeze(2).to_broadcast([T, E, E])
            nc.vector.tensor_tensor(gt[:, :, :], other, own, ALU.is_gt).then_inc(gate_s, 1)
            nc.vector.tensor_tensor(eq[:, :, :], other, own, ALU.is_equal).then_inc(gate_s, 1)
            dve.wait_ge(gate_s, 5)
            nc.vector.tensor_tensor(eqt[:, :, :].rearrange("p a b -> p (a b)"), eq[:, :, :].rearrange("p a b -> p (a b)"),
                                    b_("tri", T), ALU.mult).then_inc(gate_s, 1)
            dve.wait_ge(gate_s, 6)
            nc.vector.tensor_tensor(ahead[:, :, :], gt[:, :, :], eqt[:, :, :], ALU.add).then_inc(gate_s, 1)
            dve.wait_ge(gate_s, 7)
            nc.vector.tensor_reduce(rank[:, :], ahead[:, :, :], AX.X, ALU.add).then_inc(gate_s, 1)
            low_hidden(0)
            dve.wait_ge(gate_s, 8)
            dve.wait_ge(lexp_done, 1)
            nc.vector.scalar_tensor_tensor(out=sel2[:, :], in0=rank[:, :], scalar=2.0, in1=lexp[:, :],
                                           op0=ALU.is_lt, op1=ALU.mult).then_inc(gate_s, 1)
            dve.wait_ge(gate_s, 9)
            nc.vector.tensor_reduce(den[:, :], sel2[:, :], AX.X, ALU.add).then_inc(gate_s, 1)
            dve.wait_ge(gate_s, 10)
            nc.vector.reciprocal(rden[:, :], den[:, :]).then_inc(gate_s, 1)
            low_hidden(1)
            dve.wait_ge(gate_s, 11)
            nc.vector.scalar_tensor_tensor(
                out=gdiag[:, :, :], in0=sel2[:, :].unsqueeze(2).to_broadcast([T, E, T]), scalar=rden[:, 0:1],
                in1=ident[0:T, 0:T].unsqueeze(1).to_broadcast([T, E, T]), op0=ALU.mult, op1=ALU.mult
            ).then_inc(gdiag_done, 1)
            for b in range(2, 4):
                low_hidden(b)
            dve.wait_ge(gall_done, 1)
            for n in range(2):
                half = slice(E // 2 * n, E // 2 * n + E // 2)
                dve.wait_ge(eo_ps, n + 1)
                nc.vector.tensor_tensor(gated[:, half, :].rearrange("p e t -> p (e t)"),
                                        bank(7 - n)[:, E // 2 * T * n:E // 2 * T * (n + 1)],
                                        gall[:, half, :].rearrange("p e t -> p (e t)"), ALU.mult).then_inc(gated_done, 1)
                dve.wait_ge(gated_done, n + 1)
                nc.vector.tensor_reduce(ysum[:, n, :], gated[:, half, :].rearrange("p e t -> p t e"), AX.X,
                                        ALU.add).then_inc(ysum_done, 1)
            dve.wait_ge(y_ps, 1)
            nc.vector.tensor_copy(y[:, :], y_bank).then_inc(y_done, 1)

        def load_context(engine, c):
            engine.dma_start(ctxT[:, CK * c:CK * c + CK], ctx_in[:, CK * c:CK * c + CK]).then_inc(ctx_in_s[c], 16)

        @block.sync
        def _(sp):
            def stack_keys(g, c, par):
                k = kparts_dram[GD * g:GD * g + GD, :, CK * c:CK * c + CK]
                src = bass.AP(k.tensor, k.offset, [[0, 2], [S, 2 * GD], [1, CK]])
                sp.dma_start(kst[0:STK, par, CK * c:CK * c + CK], src).then_inc(kst_in[par][c], 16)

            def spread_keys(c):
                sp.dma_start(kparts_dram[:, :, CK * c:CK * c + CK],
                             kparts[:, :, CK * c:CK * c + CK]).then_inc(k_out[c], 16)

            A_WQ = A_FIRST + 2 * D
            for s0, s1, s in ((0, A_FIRST, a_in_s), (A_FIRST, A_WQ, wk_in), (A_WQ, A_N, wq_in)):
                sp.dma_start(wa[:, s0:s1], a_in[:, s0:s1]).then_inc(s, 16)
            for c in range(2, CHUNKS):
                load_context(sp, c)
            for c in range(CHUNKS):
                sp.wait_ge(klo_done, 2 * c + 2)
                k = slice(CK * c, CK * c + CK)
                for n in range(2):
                    sp.dma_start(kst[2 * GD * n:2 * GD * n + 2 * GD, 0, k],
                                 kparts[0:GD, :, k]).then_inc(kst_in[0][c], 16)
                if c > 0:
                    spread_keys(c - 1)
            spread_keys(CHUNKS - 1)
            for c in range(CHUNKS):
                sp.wait_ge(k_out[c], 16)
                stack_keys(1, c, 1)
                if c == 2:
                    sp.wait_ge(ones_set, 1)
                    sp.wait_ge(act_done, len(UNITS))
                    sp.dma_start(vcur[:, 0, :, :], vall[:, 0, :, :]).then_inc(v_in[0], 16)
            sp.dma_start(vcur[:, 1, :, :], vall[:, 1, :, :]).then_inc(v_in[1], 16)
            sp.dma_start(wb[:, :], b_in).then_inc(b_in_s, 16)
            sp.dma_start(wd[:, :], d_in).then_inc(d_in_s, 16)
            for g in range(GROUPS - 2):
                for c in range(CHUNKS):
                    sp.wait_ge(lg_full, entry_no(g, c, EPC))
                    stack_keys(g + 2, c, g % 2)
                sp.wait_ge(probs_free, products_done(g))
                sp.dma_start(vcur[:, g % 2, :, :], vall[:, g + 2, :, :]).then_inc(v_in[g % 2], 16)
            sp.wait_ge(rel_sb, 1)
            sp.dma_start(bias_scratch, relT[:, :]).then_inc(rel_out, 16)
            sp.wait_ge(rel_out, 16)
            n = 2 * T - 1
            for half in range(2):
                src = bass.AP(bias_scratch.tensor, bias_scratch.offset + half * (H // 2) * n,
                              [[1, T], [n, H // 2], [1, T]])
                sp.dma_start(relb[T * half:T * half + T, :, :], src).then_inc(rel_in, 16)
            sp.wait_ge(y_done, 1)
            sp.dma_start(out, y[:, :]).then_inc(out_done, 16)
            sp.wait_ge(out_done, 16)

        @block.gpsimd
        def _(pool):
            nc.gpsimd.memset(power[:, :], -0.5).then_inc(power_set, 1)
            nc.gpsimd.memset(qs[STK:P, :, :].rearrange("p g n -> p (g n)").bitcast(U32), 0).then_inc(qs_zero, 1)
            pool.wait_ge(power_set, 1)
            deviation(pool, 0)
            nc.gpsimd.memset(kst[STK:P, 1, :].bitcast(F32), MPAIR).then_inc(kst_set, 1)
            pool.wait_ge(qsplit, 2)
            nc.gpsimd.tensor_tensor(qparts[STK // 2:STK, :, :], qf[STK // 2:STK, :, :], qparts[STK // 2:STK, :, :],
                                    ALU.subtract).then_inc(qsplit, 1)
            pool.wait_ge(qsplit, 3)
            for g0, g1, done in ((0, 1, q0_done), (1, GROUPS, q_done)):
                nc.gpsimd.tensor_tensor(
                    qs[0:STK, g0:g1, :].rearrange("p g (a t) -> p g a t", a=4),
                    qparts[:, g0:g1, :].unsqueeze(2).to_broadcast([STK, g1 - g0, 4, T]),
                    a_("maskq")[0:STK, :].unsqueeze(1).unsqueeze(3).to_broadcast([STK, g1 - g0, 4, T]),
                    ALU.mult).then_inc(done, 1)
            pool.wait_ge(kst_set, 2)
            nc.gpsimd.memset(vall[:, :, :, :].rearrange("p g t (h v) -> p (g t h) v", v=VW)[:, :, HD:VW],
                             1.0).then_inc(ones_set, 1)
            nc.gpsimd.memset(vbd[:, :, :].rearrange("p a v -> p (a v)"), 0.0).then_inc(vbd_zero, 1)
            nc.gpsimd.memset(rspread[:, :, :, :].rearrange("p m h v -> p (m h v)"), 0.0).then_inc(rspread_zero, 1)
            nc.gpsimd.memset(spare2[:, :], 0.0).then_inc(probs_free, PROBS)
            nc.gpsimd.memset(unscale[:, :], 1.0 / WSCALE ** 2).then_inc(unscale_set, 1)
            for c in range(CHUNKS):
                pool.wait_ge(k_out[c], 16)
            pool.wait_ge(unscale_set, 1)
            pool.wait_ge(act_done, 4 * CHUNKS)

            def load(n):
                p, k0, k1 = SPLITS[n]
                pool.dma_start(stage[:, n % 2, 0:k1 - k0], (w1_in, w2_in)[p][:, k0:k1]).then_inc(w_in[n % 2], 16)

            load(0)
            load(1)
            for n, (p, k0, k1) in enumerate(SPLITS):
                part = (w1p, w2p)[p]
                w = stage[:, n % 2, 0:k1 - k0]
                pool.wait_ge(w_in[n % 2], 16 * (n // 2 + 1))
                nc.gpsimd.tensor_scalar(w, w, WSCALE, None, ALU.mult).then_inc(w_scaled, 1)
                pool.wait_ge(w_scaled, n + 1)
                nc.gpsimd.tensor_copy(part[:, 0, k0:k1], w).then_inc(w_high, 1)
                pool.wait_ge(w_high, n + 1)
                nc.gpsimd.tensor_tensor(part[:, 1, k0:k1], w, part[:, 0, k0:k1], ALU.subtract).then_inc(w_split, 1)
                if n + 2 < len(SPLITS):
                    pool.wait_ge(w_split, n + 1)
                    load(n + 2)
            nb = N_BIAS - D
            rows, low = slice(0, 2 * BLK), slice(BLK, 2 * BLK)
            pool.wait_ge(d_in_s, 16)
            pool.wait_ge(w_split, len(SPLITS))
            nc.gpsimd.memset(bparts[:, :].bitcast(U32), 0).then_inc(bias_s, 1)
            nc.gpsimd.memset(spread16[:, :].bitcast(U32), 0).then_inc(bias_s, 1)
            nc.gpsimd.tensor_scalar(bscaled[:, 0:nb], d_("biases", 2 * BLK)[:, 0:nb], WSCALE, None,
                                    ALU.mult).then_inc(bias_s, 1)
            nc.gpsimd.tensor_scalar(bscaled[:, nb:N_BIAS], d_("biases", 2 * BLK)[:, nb:N_BIAS], WSCALE ** 2, None,
                                    ALU.mult).then_inc(bias_s, 1)
            pool.wait_ge(bias_s, 4)
            nc.gpsimd.tensor_copy(spread16[rows, :], d_("spread", 2 * BLK)).then_inc(bias_s, 1)
            nc.gpsimd.tensor_copy(bparts[rows, :], bscaled[:, :]).then_inc(bias_s, 1)
            pool.wait_ge(bias_s, 6)
            nc.gpsimd.tensor_tensor(bparts[low, :], bscaled[low, :], bparts[low, :],
                                    ALU.subtract).then_inc(biases_split, 1)
            pool.wait_ge(biases_split, 1)
            for n in (1, 2):
                deviation(pool, n)

        @block.scalar
        def _(act):
            for c in range(2):
                load_context(act, c)
            act.wait_ge(table_in, 1)
            nc.scalar.activation(spare[:, :], spare[:, :], ACT.Exp)
            act.wait_ge(wk_done, 2)
            for i, (kind, u) in enumerate(UNITS):
                act.wait_ge(lg_full, i + 1)
                if kind == "k":
                    nc.scalar.activation(kparts[:, 0, HALF * u:HALF * u + HALF], bank(UNIT_BANK[i])[:, 0:HALF],
                                         ACT.Identity, bias=bk16[:, :]).then_inc(act_done, 1)
                else:
                    t0, nt = value_tiles(u)
                    for t in range(nt):
                        last = nc.scalar.copy(
                            vall[:, :, t0 + t, :].rearrange("p g (h v) -> p g h v", v=VW)[:, :, :, 0:HD],
                            bank(UNIT_BANK[i])[:, P * t:P * t + P].rearrange("p (g h v) -> p g h v", g=GROUPS, v=HD))
                    last.then_inc(act_done, 1)
                if (kind, u) == ("k", 4):
                    act.wait_ge(q_read, 1)
                    nc.scalar.copy(qparts[:, :, :], qf[:, :, :]).then_inc(qsplit, 1)

            def max_row(g):
                act.wait_ge(lg_full, entry_no(g - 1, CHUNKS, 1))
                nc.scalar.copy(qs[STK:STK + 1, bass.ds(g, 1), :].rearrange("p g n -> p (g n)"),
                               ring[0:1, MROW % RING, 0:COLS]).then_inc(act_done, 1)

            def slot(g, par, last):
                for c in range(CHUNKS):
                    for e in range(EPC):
                        k = EPC * c + e
                        n = COLS * ENTRY_TILES[e]
                        act.wait_ge(lg_full, entry_no(g, c, e + 1))
                        act.wait_ge(probs_free, EPC * CHUNKS * g + k + 1)
                        src = last_logits(k) if last else ring[:, k % RING, :]
                        nc.scalar.activation(probs[:, k % PROBS, 0:n], src[:, 0:n], ACT.Exp,
                                             scale=SUB ** -0.5 / MSCALE).then_inc(act_done, 1)
                if not last:
                    max_row(g + 1)

            act.wait_ge(q_done, 1)
            max_row(0)
            with act.Fori(0, (GROUPS - 2) // 2) as it:
                for par in range(2):
                    slot(2 * it + par, par, False)
            slot(GROUPS - 2, 0, False)
            act.wait_ge(lam_s, 2)
            nc.scalar.activation(lame[:, :], lamd[:, :], ACT.Exp).then_inc(lam_e, 1)
            slot(GROUPS - 1, 1, True)
            tail_act(act)

        @block.vector
        def _(dve):
            nc.vector.memset(spare[:, :], 0.0).then_inc(table_in, 1)
            nc.vector.memset(warm[:, :].bitcast(F32), 0.0).then_inc(warm_set, 1)
            nc.vector.memset(kst[STK:P, 0, :].bitcast(F32), MPAIR).then_inc(kst_set, 1)
            dve.wait_ge(a_in_s, 16)
            nc.vector.bn_stats(stats[:, :], a_("x")[0:T, :]).then_inc(ln_s, 1)
            nc.vector.tensor_scalar(bk16[:, :], a_("bk"), SCALE_IN, None, ALU.mult).then_inc(wk_done, 1)
            dve.wait_ge(ln_s, 1)
            nc.vector.bn_aggr(mv[:, :], stats[:, :]).then_inc(ln_s, 1)
            dve.wait_ge(ln_s, 2)
            nc.vector.tensor_scalar(veps[:, :], mv[:, 1:2], EPS, None, ALU.add).then_inc(ln_s, 1)
            dve.wait_ge(wk_in, 16)
            nc.vector.tensor_scalar(wk16[:, :], a_("wk"), SCALE_IN, None, ALU.mult).then_inc(wk_done, 1)
            nc.vector.memset(acc[:, 0:COLS], 0.0).then_inc(acc_free, 1)
            nc.vector.tensor_scalar(bq16[:, :], a_("bq")[0:STK, :], SCALE_IN, None, ALU.mult).then_inc(qsplit, 1)
            nc.vector.tensor_copy(ident16[:, :], ident).then_inc(id16_done, 1)
            dve.wait_ge(ln_s, 4)
            nc.vector.tensor_scalar(xn[:, :], a_("x")[0:T, :], mv[:, 0:1], rstd[:, 0:1],
                                    ALU.subtract, ALU.mult).then_inc(xn_done, 1)

            def low_keys(u):
                i = UNITS.index(("k", u))
                dve.wait_ge(act_done, i + 1)
                nc.vector.scalar_tensor_tensor(
                    out=kparts[:, 1, HALF * u:HALF * u + HALF], in0=bank(UNIT_BANK[i])[:, 0:HALF], scalar=bk16[:, 0:1],
                    in1=kparts[:, 0, HALF * u:HALF * u + HALF], op0=ALU.add, op1=ALU.subtract).then_inc(klo_done, 1)

            def chunk_max(g, c, h, par):
                dve.wait_ge(p1_full, chunk_no(g, c, h) + 1)
                nc.vector.tensor_reduce(mx[:, par, h, c:c + 1], p1[:, h, :, 0:HALF], AX.XY,
                                        ALU.max).then_inc(p1_empty, 1)

            def group_max(g, par):
                dve.wait_ge(p1_empty, chunk_no(g, CHUNKS, 0))
                nc.vector.tensor_reduce(negmax[:, :], mx[:, par, :, :], AX.X, ALU.max,
                                        negate=True).then_inc(nm_raw, 1)
                dve.wait_ge(nm_raw, g + 1)
                nc.vector.tensor_scalar(negmax16[:, par, :], negmax[:, :], 1.0 / MSCALE, None,
                                        ALU.mult).then_inc(m_ready, 1)

            def save_sums(g):
                dve.wait_ge(probs_free, products_done(g))
                nc.vector.tensor_copy(accs[:, bass.ds(g, 1), :].rearrange("p g n -> p (g n)"),
                                      acc[:, 0:COLS]).then_inc(acc_free, 1)

            for kind, u in ORDER:
                if kind == "k":
                    low_keys(u)
                elif kind == "m":
                    for h in range(2):
                        chunk_max(0, u, h, 0)
                if (kind, u) == ("k", 1):
                    dve.wait_ge(xnT_ps, 1)
                    nc.vector.tensor_copy(xnT[:, :], p1[:, 0, 0, 0:T]).then_inc(xnT_done, 1)
                if (kind, u) == ("k", 3):
                    dve.wait_ge(q_ps, 1)
                    dve.wait_ge(qsplit, 1)
                    nc.vector.scalar_tensor_tensor(
                        out=qf[:, :, :], in0=p1[0:STK, 0, 1, :].rearrange("p (g t) -> p g t", g=GROUPS),
                        scalar=SCALE_IN, in1=bq16[:, :].unsqueeze(2).to_broadcast([STK, GROUPS, T]),
                        op0=ALU.mult, op1=ALU.add).then_inc(q_read, 1)
            group_max(0, 0)
            for h in range(2):
                chunk_max(1, 0, h, 1)

            def lambda_dots():
                dve.wait_ge(b_in_s, 16)
                nc.vector.tensor_tensor(lamp[:, :, :].rearrange("p a b -> p (a b)"), b_("lamq"), b_("lamk"),
                                        ALU.mult).then_inc(lam_s, 1)
                dve.wait_ge(lam_s, 1)
                nc.vector.tensor_reduce(lamd[:, :], lamp[:, :, :], AX.X, ALU.add).then_inc(lam_s, 1)
                nc.vector.memset(coef[0:T, :], 1.0 - LAMBDA_INIT).then_inc(coef_done, 1)
                nc.vector.tensor_tensor(xbo[:, :], a_("x")[0:T, :], b_("bo", T), ALU.add).then_inc(xbo_done, 1)

            def lambda_coefficients():
                dve.wait_ge(lam_e, 1)
                nc.vector.tensor_tensor(lamx[:, :], lame[:, 1:2], lame[:, 0:1], ALU.subtract).then_inc(lam_s, 1)
                dve.wait_ge(lam_s, 3)
                nc.vector.tensor_scalar(coef2[:, :], lamx[:, :], -LAMBDA_INIT, 1.0 - LAMBDA_INIT,
                                        ALU.add, ALU.mult).then_inc(lam_s, 1)
                dve.wait_ge(lam_s, 4)
                nc.vector.tensor_copy(coef[T:P, :], coef2[T:P, :]).then_inc(coef_done, 1)
                nc.vector.scalar_tensor_tensor(out=vbt[:, :], in0=coef2[:, :], scalar=1.0 - LAMBDA_INIT, in1=b_("vb"),
                                               op0=ALU.add, op1=ALU.mult).then_inc(vbt_done, 1)

            def slot(g, par):
                for c in range(1, CHUNKS - 1):
                    for h in range(2):
                        chunk_max(g + 1, c + 1, h, 1 - par)
                group_max(g + 1, 1 - par)
                if not (isinstance(g, int) and g == GROUPS - 2):
                    for c in range(2):
                        for h in range(2):
                            chunk_max(g + 2, c, h, par)
                save_sums(g)

            for h in range(2):
                chunk_max(1, 1, h, 1)
            with dve.Fori(0, (GROUPS - 2) // 2) as it:
                for par in range(2):
                    slot(2 * it + par, par)
            lambda_dots()
            slot(GROUPS - 2, 0)
            lambda_coefficients()
            dve.wait_ge(rel_ps, 1)
            nc.vector.tensor_copy(relT[:, :], bank(1)[0:H, 0:2 * T - 1]).then_inc(rel_sb, 1)
            save_sums(GROUPS - 1)
            tail_dve(dve)

        @block.tensor
        def _(pe):
            def project(i):
                kind, u = UNITS[i]
                dst = bank(UNIT_BANK[i])
                before = [j for j in range(i) if UNIT_BANK[j] == UNIT_BANK[i]]
                if before:
                    unit_read(pe, before[-1])
                if u % 2 == 0:
                    pe.wait_ge(ctx_in_s[u // 2], 16)
                if kind == "k":
                    last = pe.matmul(dst[:, 0:HALF], wk16[:, :], ctxT[:, HALF * u:HALF * u + HALF],
                                     start=True, stop=True)
                else:
                    t0, nt = value_tiles(u)
                    for t in range(nt):
                        k = P * (t0 + t)
                        last = pe.matmul(dst[:, P * t:P * t + P], ctxT[:, k:k + P], a_("wv"),
                                         start=True, stop=True)
                last.then_inc(lg_full, 1)

            def pass1(g, c, h, par, arrived):
                if h == 0:
                    pe.wait_ge(kst_in[par][c], arrived)
                if not (isinstance(g, int) and chunk_no(g, c, h) < 2):
                    pe.wait_ge(p1_empty, chunk_no(g, c, h) - 1)
                q = qs[:, bass.ds(g, 1), T * 2 * h:T * 2 * h + 2 * T].rearrange("p g n -> p (g n)")
                for i in range(2):
                    k = CK * c + HALF * i
                    last = pe.matmul(p1[:, h, i, 0:HALF], q, kst[:, par, k:k + HALF], start=True, stop=True)
                last.then_inc(p1_full, 1)

            def pass2(g, c, e, par, last):
                k = EPC * c + e
                ahead_by = 5 if last else RING
                dst = last_logits(k) if last else ring[:, k % RING, :]
                if k >= ahead_by:
                    pe.wait_ge(act_done, entry_no(g, c, e) - ahead_by + 1)
                elif k >= RING:
                    pe.wait_ge(p1_empty, chunk_no(GROUPS, 0, 0))
                elif k == 0:
                    pe.wait_ge(act_done, entry_no(g, 0, 0))
                q = qs[:, bass.ds(g, 1), :].rearrange("p g n -> p (g n)")
                for i in range(ENTRY_TILES[e]):
                    t = TPC * c + ENTRY0[e] + i
                    done = pe.matmul(dst[:, COLS * i:COLS * i + COLS],
                                     kst[:, par, P * t:P * t + P], q, start=True, stop=True)
                done.then_inc(lg_full, 1)

            def values(g, c, par, it):
                tiles = VALUE_TILES[c]
                if 0 in tiles:
                    pe.wait_ge(v_in[par], 16 * it + 16)
                    pe.wait_ge(acc_free, g + 1)
                for t in tiles:
                    ct, e = t // TPC, t % TPC // 2
                    k = EPC * ct + e
                    i = t - TPC * ct - ENTRY0[e]
                    if i == 0 or t == tiles[0]:
                        pe.wait_ge(act_done, entry_no(g, ct, e + 1))
                    parts = 1 if t < KT - 1 else 4
                    n = COLS // parts
                    for j in range(parts):
                        row = BLK * ((t + j) % 4)
                        col = COLS * i + n * j
                        last = pe.matmul(acc[row:row + 2 * VW, n * j:n * j + n], vcur[:, par, t, :],
                                         probs[:, k % PROBS, col:col + n],
                                         start=(t < 4), stop=(t >= KT - 5), skip_group_check=True)
                    if i == ENTRY_TILES[e] - 1:
                        last.then_inc(probs_free, 1)

            def max_row(g, par):
                pe.wait_ge(m_ready, g + 1)
                pe.wait_ge(act_done, entry_no(g - 1, CHUNKS, 0) - RING + 1)
                for h in range(2):
                    last = pe.matmul(ring[0:1, MROW % RING, P * h:P * h + P], negmax16[:, par, h:h + 1],
                                     ident16[:, :], start=True, stop=True)
                last.then_inc(lg_full, 1)

            pe.wait_ge(warm_set, 1)
            for _ in range(WARM):
                pe.matmul(bank(0), warm[:, 0:P], warm[:, :], start=True, stop=True)
            pe.wait_ge(wk_done, 2)
            i = 0
            for kind, u in ORDER:
                if kind != "m":
                    project(i)
                    i += 1
                else:
                    if u == 0:
                        pe.wait_ge(q0_done, 1)
                        pe.wait_ge(qs_zero, 1)
                        pe.wait_ge(kst_set, 2)
                        for b in (2, 3):
                            unit_read(pe, max(j for j in range(WIDE) if UNIT_BANK[j] == b))
                    for h in range(2):
                        pass1(0, u, h, 0, 32)
                if (kind, u) == ("k", 1):
                    pe.wait_ge(xn_done, 1)
                    pe.transpose(p1[:, 0, 0, 0:T], xn[:, :], ident[0:T, 0:T]).then_inc(xnT_ps, 1)
                if (kind, u) == ("k", 3):
                    pe.wait_ge(wq_in, 16)
                    pe.wait_ge(xnT_done, 1)
                    for g in range(GROUPS):
                        last = pe.matmul(p1[0:STK, 0, 1, T * g:T * g + T], a_("wq")[:, STK * g:STK * g + STK],
                                         xnT[:, :], start=True, stop=True)
                    last.then_inc(q_ps, 1)
            pe.wait_ge(q_done, 1)
            for h in range(2):
                pass1(1, 0, h, 1, 16)
            pe.wait_ge(id16_done, 1)
            pe.wait_ge(act_done, len(UNITS))
            max_row(0, 0)

            def step(g, c, par, it, last, last_but_one):
                pass2(g, c, 0, par, last)
                for h in range(2):
                    pass2(g, c, 1 + h, par, last)
                    if c < CHUNKS - 1 and not last:
                        pass1(g + 1, c + 1, h, 1 - par, stacked(it, par, 1))
                    elif not last and not last_but_one:
                        pass1(g + 2, 0, h, par, stacked(it, par, 2))
                pass2(g, c, 3, par, last)

            def slot(g, par, it):
                last, last_but_one = (isinstance(g, int) and g == n for n in (GROUPS - 1, GROUPS - 2))
                for c in range(1, CHUNKS):
                    step(g, c, par, it, last, last_but_one)
                    if c == CHUNKS - 1 and not last:
                        max_row(g + 1, 1 - par)
                    values(g, c, par, it)
                    if last:
                        sums(pe, c - 1)
                if last:
                    sums(pe, CHUNKS - 1)
                else:
                    step(g + 1, 0, 1 - par, it if par == 0 else it + 1, last_but_one, False)
                values(g, 0, par, it)
                if last_but_one:
                    pe.wait_ge(d_in_s, 16)
                    pe.matmul(bank(1)[0:H, 0:2 * T - 1], d_("table", 32), d_("onehot", 32),
                              start=True, stop=True).then_inc(rel_ps, 1)

            step(0, 0, 0, 0, False, False)
            with pe.Fori(0, (GROUPS - 2) // 2) as it:
                for par in range(2):
                    slot(2 * it + par, par, it)
            for g in (GROUPS - 2, GROUPS - 1):
                slot(g, g % 2, g // 2)
            tail_pe(pe)


def _buckets():
    half, exact, far = 16, 8, 128
    out = []
    for d in range(1 - T, T):
        n = abs(d)
        large = exact + int(np.float32(np.log(np.float32(max(n, 1)) / np.float32(exact)))
                            / np.float32(np.log(far / exact)) * np.float32(half - exact))
        out.append((half if d > 0 else 0) + (n if n < exact else min(large, half - 1)))
    return out


def _pack(cols, total, rows, parts):
    a = np.zeros((rows, total), np.float32)
    for k, v in parts.items():
        a[0:v.shape[0], cols[k][0]:cols[k][1]] = v
    return a


def kernel(**inputs):
    import concourse.bacc as _bacc
    from concourse.bass_utils import run_bass_kernel_spmd as _run

    i = {k: np.asarray(v) for k, v in inputs.items()}
    L = "L0_"
    inw, inb = i[L + "xattn_in_proj_weight"].T, i[L + "xattn_in_proj_bias"]
    r = np.arange(P)
    row = np.arange(STK) % (2 * GD) // 2
    maskq = (row[:, None] // SUB == np.arange(4)[None, :])
    dims = GD * np.arange(GROUPS)[:, None] + row[None, :]
    sel = np.zeros((P, 2 * VW), np.float32)
    for j in range(4):
        sel[BLK * j + np.arange(2 * VW), np.arange(2 * VW)] = 1
    maskk = (r[:, None] // HD % (H // 2) == np.arange(H // 2)[None, :])
    maskh = (r[:, None] // T == np.arange(2)[None, :]) * HD ** -0.5
    awo = np.zeros((P, 2, D), np.float32)
    for m in range(4):
        for h2 in range(2):
            row = BLK * m + HD * h2
            for half in range(2):
                head = H // 2 * half + 2 * m + h2
                awo[row:row + HD, half] = i[L + "attn_w_o"].T[HD * head:HD * head + HD]
    awo = awo.reshape(P, 2 * D)
    tri = np.broadcast_to((np.arange(E)[None, :] < np.arange(E)[:, None]).reshape(1, E * E), (P, E * E))
    onehot = (np.arange(32)[:, None] == np.array(_buckets())[None, :])
    a = _pack(A_AT, A_N, P, dict(x=i["x"][0], ident=np.eye(P), bk=inb[D:2 * D, None], bq=inb[0:D][dims.T],
                                 maskq=maskq, wk=inw[:, D:2 * D], wv=inw[:, 2 * D:3 * D], wq=inw[:, 0:D][:, dims.ravel()]))
    b = _pack(B_AT, B_N, P, dict(
        sel=sel, vb=inb[2 * D:, None], ident2=np.tile(np.eye(T), (2, 1)),
        bo=np.broadcast_to(i[L + "xattn_out_proj_bias"], (T, D)),
        lamq=np.broadcast_to(np.concatenate([i[L + "xattn_lambda_q1"], i[L + "xattn_lambda_q2"]]), (P, 2 * SUB)),
        lamk=np.broadcast_to(np.concatenate([i[L + "xattn_lambda_k1"], i[L + "xattn_lambda_k2"]]), (P, 2 * SUB)),
        wo=i[L + "xattn_out_proj_weight"].T, awq=i[L + "attn_w_q"].T, awk=i[L + "attn_w_k"].T,
        awv=i[L + "attn_w_v"].T, awo=awo, maskk=maskk, maskh=maskh, tri=tri,
        rw2=i[L + "ffn_rw2"].reshape(FC, P, E).transpose(1, 0, 2).reshape(P, FC * E),
        flip=np.kron(np.eye(2), np.eye(T)[::-1])))
    eb1 = i[L + "ffn_eb1"].reshape(4, 2 * FC, P)
    biases, spread = np.zeros((2 * BLK, N_BIAS), np.float32), np.zeros((2 * BLK, E * T), np.float32)
    for row in (0, BLK):
        biases[row:row + E, 0:4 * P] = eb1.transpose(1, 0, 2).reshape(2 * FC, 4 * P)
        biases[row:row + FC, 4 * P:5 * P] = i[L + "ffn_rb1"].reshape(FC, P)
        biases[row:row + E, 5 * P:6 * P] = i[L + "ffn_eb2"]
        spread[row:row + E] = np.repeat(np.eye(E), T, axis=1)
    d = _pack(D_AT, D_N, 2 * BLK, dict(table=i[L + "attn_rel_bias_table"], onehot=onehot, spread=spread, biases=biases,
                                       ones=np.ones((1, P)), rb2=i[L + "ffn_rb2"].reshape(1, E)))
    arrays = dict(
        a_in=a, ctx_in=i["ctx_1024"][0].T, b_in=b,
        w1_in=np.concatenate([i[L + "ffn_rw1"], i[L + "ffn_ew1"].transpose(1, 0, 2).reshape(P, E * FH)], axis=1),
        w2_in=i[L + "ffn_ew2"].reshape(E, FC, P, D).transpose(2, 0, 1, 3).reshape(P, N2), d_in=d)
    arrays = {k: np.ascontiguousarray(v) for k, v in arrays.items()}
    nc = _bacc.Bacc("TRN2", target_bir_lowering=False, num_devices=1)
    args = [nc.dram_tensor(k, v.shape, F32, kind="ExternalInput").ap() for k, v in arrays.items()]
    scratch = nc.dram_tensor("relative_bias", (H, 2 * T - 1), F32, kind="Internal").ap()
    kparts = nc.dram_tensor("key_parts", (D, 2, S), F16, kind="Internal").ap()
    out = nc.dram_tensor("out_dram", (T, D), F32, kind="ExternalOutput").ap()
    perceiver_layer(nc, *args, scratch, kparts, out)
    got = _run(nc, [arrays], core_ids=[0])
    return got.results[0]["out_dram"].reshape(1, T, D)
```
